# Optimizing a Trainium2 kernel written in Bass

```python
import numpy as np
import jax
import jax.numpy as jnp

def _softmax(x, axis=-1):
    return jax.nn.softmax(x, axis=axis)

def _gelu(x):
    return jax.nn.gelu(x, approximate=True)

def _silu(x):
    return jax.nn.silu(x)

def _sigmoid(x):
    return jax.nn.sigmoid(x)

def _layernorm(x, axis=-1, eps=1e-05):
    m = jnp.mean(x, axis=axis, keepdims=True)
    v = jnp.var(x, axis=axis, keepdims=True)
    return (x - m) / jnp.sqrt(v + eps)

def _scatter_add(tgt, idx, src, axis=0):
    return tgt.at[idx].add(src)

def _segment_sum(src, seg, n):
    return jax.ops.segment_sum(src, seg, n)
kernel_name = 'mk_adaln_d1_jaxref_r8_78f7fc'

def setup_inputs(seed: int=0):
    np.random.seed(seed)
    _w = jnp.asarray

    def _L0_attn_setup():
        import jax, jax.numpy as jnp
        import numpy as np
        DIM = 128
        HEADS = 16
        DIM_HEAD = 64
        SOFTCLAMP = 50.0

        def _rmsnorm(x, w):
            eps = jnp.finfo(x.dtype).eps
            var = jnp.mean(jnp.square(x), axis=-1, keepdims=True)
            return x * jax.lax.rsqrt(var + eps) * w

        def _head_rmsnorm(x, gamma):
            norm = jnp.linalg.norm(x, axis=-1, keepdims=True)
            normed = x / jnp.maximum(norm, 1e-12)
            scale = (gamma + 1.0) * DIM_HEAD ** 0.5
            return normed * scale[None, :, None, :]
        key = jax.random.key(seed)
        ks = jax.random.split(key, 7)
        b, n = (4, 256)
        di = HEADS * DIM_HEAD
        s = 0.02
        return {'tokens': jax.random.normal(ks[0], (b, n, DIM), dtype=jnp.float32), 'norm_w': jnp.ones((DIM,), dtype=jnp.float32), 'Wq': jax.random.normal(ks[1], (DIM, di), dtype=jnp.float32) * s, 'Wkv': jax.random.normal(ks[2], (DIM, 2 * di), dtype=jnp.float32) * s, 'Wo': jax.random.normal(ks[3], (di, DIM), dtype=jnp.float32) * s, 'q_gamma': jnp.zeros((HEADS, DIM_HEAD), dtype=jnp.float32), 'k_gamma': jnp.zeros((HEADS, DIM_HEAD), dtype=jnp.float32)}
    _L0_attn_in = _L0_attn_setup()

    def _L0_ffn_setup():
        import jax, jax.numpy as jnp
        import numpy as np
        B, S, H = (1, 256, 128)
        E, K = (16, 4)
        G, TG = (4, 2)
        I_MOE = 64
        N_SH = 2
        SCALE = 2.5

        def _mlp(x, gw, uw, dw):
            return jax.nn.silu(x @ gw.T) * (x @ uw.T) @ dw.T

        def _route(x2d, router_weight, e_bias):
            T = x2d.shape[0]
            scores = jax.nn.sigmoid(x2d @ router_weight.T)
            sc = scores + e_bias[None, :]
            group_scores = jnp.sum(jax.lax.top_k(sc.reshape(T, G, E // G), 2)[0], axis=-1)
            _, gidx = jax.lax.top_k(group_scores, TG)
            gmask = jnp.zeros((T, G), sc.dtype).at[jnp.arange(T)[:, None], gidx].set(1.0)
            smask = jnp.repeat(gmask, E // G, axis=1)
            masked = jnp.where(smask > 0, sc, 0.0)
            _, tidx = jax.lax.top_k(masked, K)
            tw = jnp.take_along_axis(scores, tidx, axis=1)
            tw = tw / (jnp.sum(tw, axis=-1, keepdims=True) + 1e-20)
            tw = tw * SCALE
            return (tidx, tw)

        def _moe_forward(hidden_states, router_weight, e_bias, gate_w, up_w, down_w, sh_gate_w, sh_up_w, sh_down_w):
            orig_shape = hidden_states.shape
            x = hidden_states.reshape(-1, H)
            T = x.shape[0]
            tidx, tw = _route(x, router_weight, e_bias)
            g = jnp.einsum('th,eih->tei', x, gate_w)
            u = jnp.einsum('th,eih->tei', x, up_w)
            h = jax.nn.silu(g) * u
            yo = jnp.einsum('tei,ehi->teh', h, down_w)
            combine = jnp.zeros((T, E), tw.dtype).at[jnp.arange(T)[:, None], tidx].add(tw)
            routed = jnp.einsum('te,teh->th', combine, yo)
            shared = _mlp(hidden_states.reshape(-1, H), sh_gate_w, sh_up_w, sh_down_w)
            return (routed + shared).reshape(orig_shape)
        key = jax.random.key(seed)
        ks = jax.random.split(key, 9)
        s = 0.02
        return {'hidden_states': jax.random.normal(ks[0], (B, S, H), jnp.float32), 'router_weight': jax.random.normal(ks[1], (E, H), jnp.float32) * s, 'e_bias': jnp.zeros((E,), jnp.float32), 'gate_w': jax.random.normal(ks[2], (E, I_MOE, H), jnp.float32) * s, 'up_w': jax.random.normal(ks[3], (E, I_MOE, H), jnp.float32) * s, 'down_w': jax.random.normal(ks[4], (E, H, I_MOE), jnp.float32) * s, 'sh_gate_w': jax.random.normal(ks[5], (N_SH * I_MOE, H), jnp.float32) * s, 'sh_up_w': jax.random.normal(ks[6], (N_SH * I_MOE, H), jnp.float32) * s, 'sh_down_w': jax.random.normal(ks[7], (H, N_SH * I_MOE), jnp.float32) * s}
    _L0_ffn_in = _L0_ffn_setup()
    _L0_c = _w((lambda *s: np.random.randn(*s).astype(np.float32) * 0.05)(8, 128))
    _L0_wmod = _w((lambda *s: np.random.randn(*s).astype(np.float32) * 0.05)(128, 6 * 128) * 128 ** (-0.5))
    _d = {'L0_attn_tokens': _L0_attn_in['tokens'], 'L0_attn_norm_w': _L0_attn_in['norm_w'], 'L0_attn_Wq': _L0_attn_in['Wq'], 'L0_attn_Wkv': _L0_attn_in['Wkv'], 'L0_attn_Wo': _L0_attn_in['Wo'], 'L0_attn_q_gamma': _L0_attn_in['q_gamma'], 'L0_attn_k_gamma': _L0_attn_in['k_gamma'], 'L0_ffn_router_weight': _L0_ffn_in['router_weight'], 'L0_ffn_e_bias': _L0_ffn_in['e_bias'], 'L0_ffn_gate_w': _L0_ffn_in['gate_w'], 'L0_ffn_up_w': _L0_ffn_in['up_w'], 'L0_ffn_down_w': _L0_ffn_in['down_w'], 'L0_ffn_sh_gate_w': _L0_ffn_in['sh_gate_w'], 'L0_ffn_sh_up_w': _L0_ffn_in['sh_up_w'], 'L0_ffn_sh_down_w': _L0_ffn_in['sh_down_w'], 'L0_c': _L0_c, 'L0_wmod': _L0_wmod}
    _x0 = _d['L0_attn_tokens']
    _d['L0_attn_tokens'] = jax.random.normal(jax.random.fold_in(jax.random.key(seed), 1), (8, 512, 128), dtype=_x0.dtype)
    del _x0
    return _d

def reference(L0_attn_tokens, L0_attn_norm_w, L0_attn_Wq, L0_attn_Wkv, L0_attn_Wo, L0_attn_q_gamma, L0_attn_k_gamma, L0_ffn_router_weight, L0_ffn_e_bias, L0_ffn_gate_w, L0_ffn_up_w, L0_ffn_down_w, L0_ffn_sh_gate_w, L0_ffn_sh_up_w, L0_ffn_sh_down_w, L0_c, L0_wmod):

    def _L0_attn_ref(tokens, norm_w, Wq, Wkv, Wo, q_gamma, k_gamma):
        import jax, jax.numpy as jnp
        import numpy as np
        DIM = 128
        HEADS = 16
        DIM_HEAD = 64
        SOFTCLAMP = 50.0

        def _rmsnorm(x, w):
            eps = jnp.finfo(x.dtype).eps
            var = jnp.mean(jnp.square(x), axis=-1, keepdims=True)
            return x * jax.lax.rsqrt(var + eps) * w

        def _head_rmsnorm(x, gamma):
            norm = jnp.linalg.norm(x, axis=-1, keepdims=True)
            normed = x / jnp.maximum(norm, 1e-12)
            scale = (gamma + 1.0) * DIM_HEAD ** 0.5
            return normed * scale[None, :, None, :]
        b, n, _ = tokens.shape
        x = _rmsnorm(tokens, norm_w)
        q = x @ Wq
        kv = x @ Wkv
        k, v = jnp.split(kv, 2, axis=-1)
        split = lambda t: t.reshape(b, n, HEADS, DIM_HEAD).transpose(0, 2, 1, 3)
        q, k, v = (split(q), split(k), split(v))
        q = _head_rmsnorm(q, q_gamma)
        k = _head_rmsnorm(k, k_gamma)
        sim = jnp.einsum('bhid,bhjd->bhij', q, k)
        sim = jnp.tanh(sim / SOFTCLAMP) * SOFTCLAMP
        sim = sim * DIM_HEAD ** (-0.5)
        attn = jax.nn.softmax(sim, axis=-1)
        out = jnp.einsum('bhij,bhjd->bhid', attn, v)
        out = out.transpose(0, 2, 1, 3).reshape(b, n, HEADS * DIM_HEAD)
        return out @ Wo

    def _L0_ffn_ref(hidden_states, router_weight, e_bias, gate_w, up_w, down_w, sh_gate_w, sh_up_w, sh_down_w):
        import jax, jax.numpy as jnp
        import numpy as np
        B, S, H = (1, 256, 128)
        E, K = (16, 4)
        G, TG = (4, 2)
        I_MOE = 64
        N_SH = 2
        SCALE = 2.5

        def _mlp(x, gw, uw, dw):
            return jax.nn.silu(x @ gw.T) * (x @ uw.T) @ dw.T

        def _route(x2d, router_weight, e_bias):
            T = x2d.shape[0]
            scores = jax.nn.sigmoid(x2d @ router_weight.T)
            sc = scores + e_bias[None, :]
            group_scores = jnp.sum(jax.lax.top_k(sc.reshape(T, G, E // G), 2)[0], axis=-1)
            _, gidx = jax.lax.top_k(group_scores, TG)
            gmask = jnp.zeros((T, G), sc.dtype).at[jnp.arange(T)[:, None], gidx].set(1.0)
            smask = jnp.repeat(gmask, E // G, axis=1)
            masked = jnp.where(smask > 0, sc, 0.0)
            _, tidx = jax.lax.top_k(masked, K)
            tw = jnp.take_along_axis(scores, tidx, axis=1)
            tw = tw / (jnp.sum(tw, axis=-1, keepdims=True) + 1e-20)
            tw = tw * SCALE
            return (tidx, tw)

        def _moe_forward(hidden_states, router_weight, e_bias, gate_w, up_w, down_w, sh_gate_w, sh_up_w, sh_down_w):
            orig_shape = hidden_states.shape
            x = hidden_states.reshape(-1, H)
            T = x.shape[0]
            tidx, tw = _route(x, router_weight, e_bias)
            g = jnp.einsum('th,eih->tei', x, gate_w)
            u = jnp.einsum('th,eih->tei', x, up_w)
            h = jax.nn.silu(g) * u
            yo = jnp.einsum('tei,ehi->teh', h, down_w)
            combine = jnp.zeros((T, E), tw.dtype).at[jnp.arange(T)[:, None], tidx].add(tw)
            routed = jnp.einsum('te,teh->th', combine, yo)
            shared = _mlp(hidden_states.reshape(-1, H), sh_gate_w, sh_up_w, sh_down_w)
            return (routed + shared).reshape(orig_shape)
        return _moe_forward(hidden_states, router_weight, e_bias, gate_w, up_w, down_w, sh_gate_w, sh_up_w, sh_down_w)
    x = L0_attn_tokens
    mod = (_silu(L0_c) @ L0_wmod).reshape(L0_c.shape[0], 6, 1, -1)
    sa, ca, ga, sb, cb, gb = (mod[:, 0], mod[:, 1], mod[:, 2], mod[:, 3], mod[:, 4], mod[:, 5])
    ga = (2 * (ga >= 0) - 1) * jnp.maximum(jnp.abs(ga), 0.25)
    gb = (2 * (gb >= 0) - 1) * jnp.maximum(jnp.abs(gb), 0.25)
    h = _layernorm(x, axis=-1) * (1 + ca) + sa
    x = x + ga * _L0_attn_ref(h, L0_attn_norm_w, L0_attn_Wq, L0_attn_Wkv, L0_attn_Wo, L0_attn_q_gamma, L0_attn_k_gamma)
    h = _layernorm(x, axis=-1) * (1 + cb) + sb
    x = x + gb * _L0_ffn_ref(h, L0_ffn_router_weight, L0_ffn_e_bias, L0_ffn_gate_w, L0_ffn_up_w, L0_ffn_down_w, L0_ffn_sh_gate_w, L0_ffn_sh_up_w, L0_ffn_sh_down_w)
    return x

_drawn_inputs = setup_inputs


def setup_inputs(seed=0):
    import zlib

    import numpy as np

    out = dict(_drawn_inputs(seed))
    spreads = {'L0_attn_norm_w': (1.0, 0.6),
     'L0_attn_q_gamma': (0.0, 0.8),
     'L0_attn_k_gamma': (0.0, 0.8),
     'L0_ffn_e_bias': (0.0, 0.8)}
    factors = {'L0_attn_Wq': 8.0,
     'L0_attn_Wkv': 8.0,
     'L0_attn_Wo': 8.0,
     'L0_ffn_router_weight': 8.0,
     'L0_ffn_gate_w': 8.0,
     'L0_ffn_up_w': 8.0,
     'L0_ffn_down_w': 8.0,
     'L0_ffn_sh_gate_w': 8.0,
     'L0_ffn_sh_up_w': 8.0,
     'L0_ffn_sh_down_w': 8.0,
     'L0_c': 8.0,
     'L0_wmod': 8.0}
    for name, (base, spread) in spreads.items():
        noise = np.random.default_rng([zlib.crc32(name.encode()), seed]).standard_normal(out[name].shape)
        drawn = base * np.exp(spread * noise) if base else spread * noise
        out[name] = jnp.asarray(drawn.astype(out[name].dtype))
    for name, factor in factors.items():
        out[name] = (out[name] * factor).astype(out[name].dtype)
    return out
```

```python
from contextlib import ExitStack

import concourse.bass as bass
from concourse import mybir

F32 = mybir.dt.float32
F16 = mybir.dt.float16
I32 = mybir.dt.int32
ALU = mybir.AluOpType
ACT = mybir.ActivationFunctionType
AX_X = mybir.AxisListType.X

P = 128
NB = 8
SEQ = 512
NT = SEQ // P
HEADS = 16
DH = 64
HD = HEADS * DH
PAIRS = HEADS // 2
E = 16
NG = 4
EG = E // NG
TOPK = 4
TOPG = 2
I_MOE = 64
NJ = E * I_MOE // P + 1
SOFTCLAMP = 50.0
QSCALE = DH ** 0.5
LN_EPS = 1e-5
RMS_EPS = 1.1920928955078125e-07
NORM_MIN = 1e-12
ROUTE_SCALE = 2.5
GATE_MIN = 0.25
MAGIC = 1597463007.0


def block_kernel(nc, x, wqkv, wo, wg, wu, wd, wr, gq, gk, nw, ebias, cT, wmod, out):
    ctx = ExitStack()
    with ctx:
        def sb(name, shape, dt=F32):
            return ctx.enter_context(nc.sbuf_tensor(name, shape, dt))

        def ps(name, shape, dt=F32):
            return ctx.enter_context(nc.psum_tensor(name, shape, dt))

        sems = []

        def sem(name):
            s = ctx.enter_context(nc.semaphore(name))
            sems.append(s)
            return s

        wqkv_sb = sb("wqkv_sb", [P, 3 * HD])
        wo_sb = sb("wo_sb", [P, PAIRS, P])
        wg_sb = sb("wg_sb", [P, NJ, P])
        wu_sb = sb("wu_sb", [P, NJ, P])
        wd_sb = sb("wd_sb", [P, NJ, P])
        wr_sb = sb("wr_sb", [P, E])
        gam = sb("gam", [P, HD])
        gq_sb = sb("gq_sb", [P, HD])
        nw_sb = sb("nw_sb", [P, 1])
        eb_sb = sb("eb_sb", [P, E])
        c_sb = sb("c_sb", [P, NB])
        cth = sb("cth", [P, NB])
        wmod_sb = sb("wmod_sb", [P, 6, P])
        modT = sb("modT", [P, 6, NB])
        mtmp = sb("mtmp", [P, 2, NB])
        ident = sb("ident", [P, P])
        ident16 = sb("ident16", [P, P], F16)
        ones = sb("ones", [P, 1])
        expand = sb("expand", [P, NJ - 1, P], F16)
        lt = sb("lt", [P, NG, NG])

        x_sb = sb("x_sb", [P, NT, P])
        mod = sb("mod", [P, 6])
        st = sb("st", [P, NT, 6])
        mv = sb("mv", [P, NT, 2])
        xh = sb("xh", [P, NT, P])
        hT = sb("hT", [P, SEQ])
        sqT = sb("sqT", [P, SEQ])
        r1 = sb("r1", [P, NT])
        nx = sb("nx", [P, 2 * HEADS])
        ny = sb("ny", [P, 2 * HEADS])
        nt_ = sb("nt_", [P, 2 * HEADS])
        QT = sb("QT", [P, HEADS, SEQ], F16)
        KT = sb("KT", [P, HEADS, SEQ], F16)
        KS = sb("KS", [P, HEADS, SEQ], F16)
        Vh = sb("Vh", [P, NT, HEADS, DH + 1], F16)
        Vl = sb("Vl", [P, NT, HEADS, DH], F16)
        pr = sb("pr", [P, 3, NT, SEQ])
        parts = sb("parts", [P, 4, NT, SEQ], F16)
        ph, pl = parts[:, 0:2], parts[:, 2:4]
        qk = pr[:, 0:2].rearrange("p s a q -> p s (a q)")
        sq = pr[:, 2].rearrange("p a q -> p (a q)")
        qks = parts[:].rearrange("p (s r) a q -> p s (r a q)", s=2).rearrange(
            "p s (h r d) -> p s h r d", r=2, d=DH)
        rd = sb("rd", [P, 2, NT])
        O_sb = sb("O_sb", [P, NT, HD])
        OT = sb("OT", [P, 2, SEQ])
        aT = sb("aT", [P, SEQ])
        x1 = sb("x1", [P, NT, P])
        ex = sb("ex", [P, NT, E])
        sco = sb("sco", [P, NT, E])
        scb = sb("scb", [P, NT, E])
        g1 = sb("g1", [P, NT, NG, 4])
        gs = sb("gs", [P, NT, NG])
        bt = sb("bt", [P, NT, NG, NG])
        bt2 = sb("bt2", [P, NT, NG, NG])
        gm = sb("gm", [P, NT, NG])
        top = sb("top", [P, NT, 8])
        sel = sb("sel", [P, NT, E])
        eq = sb("eq", [P, 2, NT, 2 * E])
        need = sb("need", [P, NT])
        cmb = sb("cmb", [P, NT, E])
        cs = sb("cs", [P, NT, 2, E], F16)
        cT_sb = sb("cT_sb", [P, SEQ], F16)
        th = sb("th", [P, 2, SEQ])
        ga_ = sb("ga_", [P, 2, SEQ])
        hj = sb("hj", [P, 2, SEQ])
        o_sb = sb("o_sb", [P, NT, P])

        S = [ps(f"S{i}", [P, 2, SEQ]) for i in range(2)]
        O = [ps(f"O{i}", [P, SEQ]) for i in range(2)]
        M6 = ps("M6", [P, SEQ])
        M7 = ps("M7", [P, SEQ])
        T16 = [M6[:, :].bitcast(F16).rearrange("p (h t) -> p h t", t=P),
               M7[:, :].bitcast(F16).rearrange("p (h t) -> p h t", t=P)]

        load = ctx.enter_context(nc.semaphore("load"))
        built = ctx.enter_context(nc.semaphore("built"))
        vec0 = ctx.enter_context(nc.semaphore("vec0"))
        silu_c = ctx.enter_context(nc.semaphore("silu_c"))
        modp = ctx.enter_context(nc.semaphore("modp"))
        LOADS = 13
        with nc.Block() as block:
            @block.sync
            def _(sp):
                for dst, src in ((c_sb[:], cT), (wmod_sb[:], wmod), (wqkv_sb[:], wqkv), (nw_sb[:], nw),
                                 (gam[:], gk.to_broadcast((P, HD))), (gq_sb[:], gq.to_broadcast((P, HD))),
                                 (eb_sb[:], ebias.to_broadcast((P, E))), (wo_sb[:], wo), (wr_sb[:], wr),
                                 (wg_sb[:], wg), (wu_sb[:], wu), (wd_sb[:], wd)):
                    sp.dma_start(dst, src).then_inc(load, 16)

            @block.gpsimd
            def _(pool):
                pool.memset(ident[:], 0.0).then_inc(built, 1)
                pool.memset(expand[:], 1.0).then_inc(built, 1)
                pool.memset(lt[:], 1.0).then_inc(built, 1)
                pool.memset(ones[:], 1.0).then_inc(built, 1)
                pool.memset(eq[:], 0.0).then_inc(built, 1)
                pool.memset(cT_sb[:], 0.0).then_inc(built, 1)
                pool.memset(Vh[:], 1.0).then_inc(built, 1)
                pool.wait_ge(built, 7)
                pool.affine_select(out=ident[:], in_=ident[:], compare_op=ALU.not_equal, fill=1.0,
                                   base=0, pattern=[[-1, P]], channel_multiplier=1).then_inc(built, 1)
                pool.memset(sq[:, 0:HD], 0.0).then_inc(built, 1)
                pool.wait_ge(built, 9)
                for r in range(2):
                    v = sq[:, 0:HD].rearrange("p (e i) -> p e i", i=I_MOE)
                    pool.affine_select(out=v, in_=v, compare_op=ALU.not_equal, fill=1.0,
                                       base=-E * r, pattern=[[-1, E], [0, I_MOE]],
                                       channel_multiplier=1).then_inc(built, 1)
                    pool.wait_ge(built, 10 + r)
                pool.affine_select(out=lt[:], in_=lt[:], compare_op=ALU.is_ge, fill=0.0,
                                   base=-1, pattern=[[1, NG], [-1, NG]],
                                   channel_multiplier=0).then_inc(built, 1)

            @block.vector
            def _(dve):
                n = [0]

                def done(ins):
                    n[0] += 1
                    ins.then_inc(vec0, 1)
                    dve.wait_ge(vec0, n[0])

                dve.wait_ge(built, 12)
                done(nc.vector.tensor_copy(ident16[:], ident[:]))
                done(nc.vector.tensor_copy(expand[:].rearrange("p j f -> p (j f)"), sq[:, 0:HD]))
                dve.wait_ge(load, 16 * (LOADS - 1))
                done(nc.vector.tensor_scalar(wqkv_sb[:], wqkv_sb[:], nw_sb[:], None, ALU.mult))
                done(nc.vector.tensor_scalar(gq_sb[:], gq_sb[:], 1.0, None, ALU.add))
                done(nc.vector.scalar_tensor_tensor(gam[:], gam[:], 1.0, gq_sb[:], ALU.add, ALU.mult))
                dve.wait_ge(silu_c, 1)
                done(nc.vector.scalar_tensor_tensor(cth[:], cth[:], 1.0, c_sb[:], ALU.add, ALU.mult))
                nc.vector.tensor_scalar(cth[:], cth[:], 0.5, None, ALU.mult).then_inc(silu_c, 1)
                dve.wait_ge(modp, 1)
                m = M6[:, 0:6 * NB].rearrange("p (j b) -> p j b", j=6)
                done(nc.vector.tensor_copy(modT[:], m))
                for j in (1, 4):
                    done(nc.vector.tensor_scalar(modT[:, j, :], modT[:, j, :], 1.0, None, ALU.add))
                for j in (2, 5):
                    g = modT[:, j, :]
                    done(nc.vector.tensor_scalar(mtmp[:, 0, :], g, 0.0, 2.0, ALU.is_ge, ALU.mult))
                    done(nc.vector.tensor_scalar(mtmp[:, 0, :], mtmp[:, 0, :], -1.0, None, ALU.add))
                    done(nc.vector.tensor_tensor(mtmp[:, 1, :], g, mtmp[:, 0, :], ALU.mult))
                    done(nc.vector.tensor_scalar(mtmp[:, 1, :], mtmp[:, 1, :], GATE_MIN, None, ALU.max))
                    done(nc.vector.tensor_tensor(g, mtmp[:, 1, :], mtmp[:, 0, :], ALU.mult))

            @block.scalar
            def _(act):
                act.wait_ge(load, 16 * (LOADS - 1))
                nc.scalar.activation(cth[:], c_sb[:], ACT.Tanh, scale=0.5).then_inc(silu_c, 1)

            @block.tensor
            def _(pe):
                pe.wait_ge(silu_c, 2)
                pe.wait_ge(load, 16 * (LOADS - 1))
                for j in range(6):
                    last = nc.tensor.matmul(M6[:, j * NB:(j + 1) * NB], wmod_sb[:, j, :], cth[:],
                                            start=True, stop=True)
                last.then_inc(modp, 1)

        x_in = sem("x_in")
        k_swap = [sem(f"k_swap{g}") for g in range(4)]
        stored = sem("stored")
        vec = sem("vec")
        xh_rdy = sem("xh_rdy")
        hT_rdy = sem("hT_rdy")
        sq_rdy = sem("sq_rdy")
        r1_rdy = sem("r1_rdy")
        v_evac = sem("v_evac")
        qn_rdy = sem("qn_rdy")
        qlo_rdy = sem("qlo_rdy")
        plo_rdy = sem("plo_rdy")
        o_rdy = sem("o_rdy")
        ot_rdy = sem("ot_rdy")
        aT_rdy = sem("aT_rdy")
        x1_rdy = sem("x1_rdy")
        h2_rdy = sem("h2_rdy")
        cs_rdy = sem("cs_rdy")
        cT_rdy = sem("cT_rdy")
        hj_rdy = sem("hj_rdy")
        yT_rdy = sem("yT_rdy")
        out_rdy = sem("out_rdy")
        xT_ps = sem("xT_ps")
        ms_ps = sem("ms_ps")
        q_ps, k_ps, v_ps = sem("q_ps"), sem("k_ps"), sem("v_ps")
        t_ps = sem("t_ps")
        s_ps = sem("s_ps")
        o_ps = sem("o_ps")
        ot_ps = sem("ot_ps")
        wo_ps = sem("wo_ps")
        at_ps = sem("at_ps")
        x2_ps = sem("x2_ps")
        lg_ps = sem("lg_ps")
        gu_ps = sem("gu_ps")
        ct_ps = sem("ct_ps")
        cb_ps = sem("cb_ps")
        dn_ps = sem("dn_ps")
        y_ps = sem("y_ps")
        qk_ev = sem("qk_ev")
        v_ev = sem("v_ev")
        t_ev = sem("t_ev")
        tanh_d = sem("tanh_d")
        exp_d = sem("exp_d")
        lg_ex = sem("lg_ex")
        th_d = sem("th_d")
        sq_d = sem("sq_d")
        qhi_d = sem("qhi_d")
        phi_d = sem("phi_d")

        with nc.Fori(0, NB) as b:
            with nc.Block() as block:
                @block.sync
                def _(sp):
                    sp.dma_start(x_sb[:], x[b].rearrange("(t p) d -> p t d", p=P)).then_inc(x_in, 16)
                    sp.wait_ge(t_ev, 4 * NT)
                    for g in range(4):
                        hs = slice(4 * g, 4 * g + 4)
                        sp.dma_start(KS[DH:P, hs, :], KT[0:DH, hs, :]).then_inc(k_swap[g], 16)
                        sp.dma_start(KS[0:DH, hs, :], KT[DH:P, hs, :]).then_inc(k_swap[g], 16)
                    sp.wait_ge(out_rdy, 1)
                    sp.dma_start(out[b].rearrange("(t p) d -> p t d", p=P), o_sb[:]).then_inc(stored, 16)
                    sp.wait_ge(stored, 16)

                @block.gpsimd
                def _(pool):
                    def squares(t):
                        pool.wait_ge(qk_ev, 2 * t + 2)
                        if t:
                            pool.wait_ge(qn_rdy, t)
                        nc.gpsimd.tensor_tensor(sq[:], qk[:, t % 2, :], qk[:, t % 2, :],
                                                ALU.mult).then_inc(sq_d, 1)

                    def high(t):
                        pool.wait_ge(qn_rdy, t + 1)
                        if t >= 2:
                            pool.wait_ge(t_ps, 4 * (t - 1))
                        nc.gpsimd.tensor_scalar(qks[:, t % 2, :, 0, :],
                                                qk[:, t % 2, :].rearrange("p (h d) -> p h d", d=DH),
                                                1.0, 0.0, ALU.mult, ALU.add).then_inc(qhi_d, 1)

                    for t in range(NT + 1):
                        if t < NT:
                            squares(t)
                        if t:
                            high(t - 1)
                    for h in range(HEADS):
                        pool.wait_ge(exp_d, h + 1)
                        if h >= 2:
                            pool.wait_ge(o_ps, h - 1)
                        nc.gpsimd.tensor_scalar(ph[:, h % 2].rearrange("p a q -> p (a q)"),
                                                pr[:, h % 3].rearrange("p a q -> p (a q)"),
                                                1.0, 0.0, ALU.mult, ALU.add).then_inc(phi_d, 1)

                @block.scalar
                def _(act):
                    act.wait_ge(r1_rdy, 1)

                    def evac(t):
                        for j, (src, ready) in enumerate(((S[0], q_ps), (S[1], k_ps))):
                            act.wait_ge(ready, t + 1)
                            if t >= 2:
                                act.wait_ge(qlo_rdy, t - 1)
                            nc.scalar.activation(qk[:, t % 2, j * HD:(j + 1) * HD],
                                                 src[:].rearrange("p a n -> p (a n)"), ACT.Copy,
                                                 scale=r1[:, t:t + 1]).then_inc(qk_ev, 1)
                        act.wait_ge(v_ps, t + 1)
                        for a in range(2):
                            last = nc.scalar.activation(
                                Vh[:, t, a * 8:a * 8 + 8, 0:DH],
                                O[a][:].rearrange("p (h d) -> p h d", d=DH), ACT.Copy,
                                scale=r1[:, t:t + 1])
                        last.then_inc(v_ev, 1)

                    def transposed(t):
                        for u in range(4):
                            act.wait_ge(t_ps, 4 * t + u + 1)
                            dst = QT if u < 2 else KT
                            h0 = 8 * (u % 2)
                            nc.scalar.activation(dst[:, h0:h0 + 8, t * P:(t + 1) * P], T16[u % 2],
                                                 ACT.Copy).then_inc(t_ev, 1)

                    for t in range(NT + 1):
                        if t < NT:
                            evac(t)
                        if t:
                            transposed(t - 1)
                    for h in range(HEADS):
                        for u in range(2):
                            act.wait_ge(s_ps, 2 * h + u + 1)
                            if h >= 3 and u == 0:
                                act.wait_ge(plo_rdy, h - 2)
                            nc.scalar.activation(pr[:, h % 3, 2 * u:2 * u + 2, :], S[u][:], ACT.Tanh,
                                                 scale=QSCALE * QSCALE / SOFTCLAMP).then_inc(tanh_d, 1)
                        act.wait_ge(tanh_d, 2 * h + 2)
                        nc.scalar.activation(pr[:, h % 3], pr[:, h % 3], ACT.Exp,
                                             scale=SOFTCLAMP * DH ** -0.5).then_inc(exp_d, 1)
                    act.wait_ge(lg_ps, 1)
                    nc.scalar.activation(ex[:].rearrange("p t e -> p (t e)"), M6[:, 0:NT * E], ACT.Exp,
                                         scale=-1.0).then_inc(lg_ex, 1)
                    for j in range(NJ):
                        act.wait_ge(gu_ps, j + 1)
                        if j >= 2:
                            act.wait_ge(hj_rdy, j - 1)
                        nc.scalar.activation(th[:, j % 2, :], S[j % 2][:, 0, :], ACT.Tanh,
                                             scale=0.5).then_inc(th_d, 1)

                @block.tensor
                def _(pe):
                    def mm(*a, **k):
                        return nc.tensor.matmul(*a, **k)

                    def transpose4(dst, src, idt):
                        for t in range(NT):
                            last = nc.tensor.transpose(dst[:, t * P:(t + 1) * P], src(t), idt[:])
                        return last

                    pe.wait_ge(xh_rdy, NT)
                    transpose4(M6, lambda t: xh[:, t, :], ident).then_inc(xT_ps, 1)
                    pe.wait_ge(sq_rdy, 1)
                    for t in range(NT):
                        last = mm(M7[:, t:t + 1], sqT[:, t * P:(t + 1) * P], ones[:], start=True, stop=True)
                    last.then_inc(ms_ps, 1)

                    def project(t):
                        hx = hT[:, t * P:(t + 1) * P]
                        for j, (dst, done) in enumerate(((S[0], q_ps), (S[1], k_ps))):
                            if t:
                                pe.wait_ge(qk_ev, 2 * t - 1 + j)
                            for a in range(2):
                                c = (2 * j + a) * SEQ
                                last = mm(dst[:, a, :], hx, wqkv_sb[:, c:c + SEQ], start=True, stop=True)
                            last.then_inc(done, 1)
                        if t:
                            pe.wait_ge(v_evac, t)
                        for a in range(2):
                            c = (4 + a) * SEQ
                            last = mm(O[a][:], hx, wqkv_sb[:, c:c + SEQ], start=True, stop=True)
                        last.then_inc(v_ps, 1)

                    def transposes(t):
                        pe.wait_ge(qhi_d, t + 1)
                        pe.wait_ge(qlo_rdy, t + 1)
                        if t == 0:
                            pe.wait_ge(r1_rdy, 1)
                        for u in range(4):
                            n = 4 * t + u
                            if n >= 2:
                                pe.wait_ge(t_ev, n - 1)
                            for i in range(8):
                                last = nc.tensor.transpose(T16[u % 2][:, i, :],
                                                           qks[:, t % 2, 8 * u + i].rearrange("p a d -> p (a d)"),
                                                           ident16[:])
                            last.then_inc(t_ps, 1)

                    for t in range(NT + 1):
                        if t < NT:
                            project(t)
                        if t:
                            transposes(t - 1)

                    def scores(h):
                        if h % 4 == 0:
                            pe.wait_ge(k_swap[h // 4], 32)
                        for u in range(2):
                            if h:
                                pe.wait_ge(tanh_d, 2 * (h - 1) + u + 1)
                            for a in range(2):
                                ks = slice((2 * u + a) * P, (2 * u + a + 1) * P)
                                mm(S[u][:, a, :], KT[:, h, ks], QT[:, h, :], start=True, stop=False)
                                last = mm(S[u][:, a, :], KS[:, h, ks], QT[:, h, :], start=False, stop=True)
                            last.then_inc(s_ps, 1)

                    def values(h):
                        pe.wait_ge(phi_d, h + 1)
                        pe.wait_ge(plo_rdy, h + 1)
                        if h >= 2:
                            pe.wait_ge(o_rdy, h - 1)
                        elif h == 0:
                            pe.wait_ge(v_evac, NT)
                        for c in range(NT):
                            o = O[h % 2][:, c * (DH + 1):(c + 1) * (DH + 1)]
                            qs = slice(c * P, (c + 1) * P)
                            for k in range(NT):
                                mm(o, ph[:, h % 2, k, qs], Vh[:, k, h, :], start=(k == 0), stop=False)
                                mm(o[:, 0:DH], ph[:, h % 2, k, qs], Vl[:, k, h, :], start=False, stop=False)
                                last = mm(o, pl[:, h % 2, k, qs], Vh[:, k, h, :], start=False,
                                          stop=(k == NT - 1))
                        last.then_inc(o_ps, 1)

                    def pair(j):
                        pe.wait_ge(o_rdy, 2 * j + 2)
                        if j:
                            pe.wait_ge(ot_rdy, j)
                        for t in range(NT):
                            last = nc.tensor.transpose(M6[:, t * P:(t + 1) * P], O_sb[:, t, j * P:(j + 1) * P],
                                                       ident[:])
                        last.then_inc(ot_ps, 1)

                    def output(j):
                        pe.wait_ge(ot_rdy, j + 1)
                        mm(M7[:], wo_sb[:, j, :], OT[:, j % 2, :], start=(j == 0),
                           stop=(j == PAIRS - 1)).then_inc(wo_ps, 1)

                    pe.wait_ge(t_ev, 4 * NT)
                    scores(0)
                    for h in range(HEADS):
                        if h + 1 < HEADS:
                            scores(h + 1)
                        values(h)
                        if h % 2 == 0 and h >= 2:
                            pair(h // 2 - 1)
                        if h % 2 and h >= 3:
                            output(h // 2 - 1)
                    pair(PAIRS - 1)
                    output(PAIRS - 1)

                    pe.wait_ge(aT_rdy, 1)
                    transpose4(M6, lambda t: aT[:, t * P:(t + 1) * P], ident).then_inc(at_ps, 1)
                    pe.wait_ge(x1_rdy, NT)
                    transpose4(M7, lambda t: xh[:, t, :], ident).then_inc(x2_ps, 1)

                    pe.wait_ge(h2_rdy, 1)
                    for t in range(NT):
                        last = mm(M6[:, t * E:(t + 1) * E], hT[:, t * P:(t + 1) * P], wr_sb[:],
                                  start=True, stop=True)
                    last.then_inc(lg_ps, 1)

                    def gate_up(j):
                        w = NJ - 1 if j == 0 else j - 1
                        if j >= 2:
                            pe.wait_ge(th_d, j - 1)
                            pe.wait_ge(hj_rdy, j - 1)
                        mm(S[j % 2][:, 0, :], wg_sb[:, w, :], hT[:], start=True, stop=True)
                        mm(S[j % 2][:, 1, :], wu_sb[:, w, :], hT[:], start=True, stop=True).then_inc(gu_ps, 1)

                    def spread(j):
                        if j >= 3:
                            pe.wait_ge(hj_rdy, j - 1)
                        mm(O[j % 2][:], expand[:, j - 1, :], cT_sb[:], start=True, stop=True).then_inc(cb_ps, 1)

                    def down(j):
                        w = NJ - 1 if j == 0 else j - 1
                        pe.wait_ge(hj_rdy, j + 1)
                        mm(M7[:], wd_sb[:, w, :], hj[:, j % 2, :], start=(j == 0),
                           stop=(j == NJ - 1)).then_inc(dn_ps, 1)

                    gate_up(0)
                    gate_up(1)
                    pe.wait_ge(cs_rdy, 1)
                    c6 = M6[:, :].bitcast(F16)
                    for t in range(NT):
                        last = nc.tensor.transpose(c6[0:2 * E, t * P:(t + 1) * P],
                                                   cs[:, t].rearrange("p a e -> p (a e)"), ident16[:])
                    last.then_inc(ct_ps, 1)
                    down(0)
                    pe.wait_ge(cT_rdy, 1)
                    spread(1)
                    for j in range(1, NJ):
                        if j + 1 < NJ:
                            gate_up(j + 1)
                            spread(j + 1)
                        down(j)
                    pe.wait_ge(yT_rdy, 1)
                    transpose4(M6, lambda t: aT[:, t * P:(t + 1) * P], ident).then_inc(y_ps, 1)

                @block.vector
                def _(dve):
                    n = [0]
                    V = nc.vector

                    def done(ins):
                        n[0] += 1
                        ins.then_inc(vec, 1)
                        dve.wait_ge(vec, n[0])

                    def inverse_root(width):
                        X, Y, T = nx[:, 0:width], ny[:, 0:width], nt_[:, 0:width]
                        done(V.tensor_single_scalar(T.bitcast(I32), X.bitcast(I32), 1, ALU.arith_shift_right))
                        done(V.tensor_scalar(Y.bitcast(I32), T.bitcast(I32), -1.0, MAGIC, ALU.mult, ALU.add))
                        for _ in range(3):
                            done(V.scalar_tensor_tensor(T, Y, -0.5, Y, ALU.mult, ALU.mult))
                            done(V.tensor_tensor(T, T, X, ALU.mult))
                            done(V.scalar_tensor_tensor(Y, T, 1.5, Y, ALU.add, ALU.mult))

                    def layernorm(src, ready):
                        for t in range(NT):
                            V.bn_stats(st[:, t, :], src[:, t, :]).then_inc(vec, 1)
                            n[0] += 1
                        dve.wait_ge(vec, n[0])
                        for t in range(NT):
                            V.bn_aggr(mv[:, t, :], st[:, t, :]).then_inc(vec, 1)
                            n[0] += 1
                        dve.wait_ge(vec, n[0])
                        done(V.tensor_scalar(nx[:, 0:NT], mv[:, :, 1], LN_EPS, None, ALU.add))
                        inverse_root(NT)
                        for t in range(NT):
                            V.tensor_scalar(xh[:, t, :], src[:, t, :], mv[:, t, 0:1], ny[:, t:t + 1],
                                            ALU.subtract, ALU.mult).then_inc(ready, 1)

                    done(V.tensor_copy(mod[:], modT[:, :, bass.ds(b, 1)].rearrange("p j b -> p (j b)")))
                    dve.wait_ge(x_in, 16)
                    layernorm(x_sb, xh_rdy)
                    dve.wait_ge(xT_ps, 1)
                    V.tensor_scalar(hT[:], M6[:], mod[:, 1:2], mod[:, 0:1], ALU.mult, ALU.add).then_inc(hT_rdy, 1)
                    dve.wait_ge(hT_rdy, 1)
                    V.tensor_tensor(sqT[:], hT[:], hT[:], ALU.mult).then_inc(sq_rdy, 1)
                    dve.wait_ge(ms_ps, 1)
                    done(V.tensor_scalar(nx[:, 0:NT], M7[:, 0:NT], 1.0 / P, RMS_EPS, ALU.mult, ALU.add))
                    inverse_root(NT)
                    V.tensor_copy(r1[:], ny[:, 0:NT]).then_inc(r1_rdy, 1)
                    dve.wait_ge(r1_rdy, 1)

                    def low_v(t):
                        dve.wait_ge(v_ev, t + 1)
                        for a in range(2):
                            hs = slice(8 * a, 8 * a + 8)
                            last = V.scalar_tensor_tensor(Vl[:, t, hs, :], O[a][:].rearrange("p (h d) -> p h d", d=DH),
                                                          r1[:, t:t + 1], Vh[:, t, hs, 0:DH],
                                                          ALU.mult, ALU.subtract)
                        last.then_inc(v_evac, 1)

                    def head_norms(t):
                        dve.wait_ge(sq_d, t + 1)
                        done(V.tensor_reduce(nx[:], sq[:].rearrange("p (h d) -> p h d", d=DH), AX_X, ALU.add))
                        done(V.tensor_scalar(nx[:], nx[:], NORM_MIN * NORM_MIN, None, ALU.max))
                        inverse_root(2 * HEADS)
                        kk = qk[:, t % 2, HD:2 * HD]
                        done(V.tensor_tensor(kk, kk, gam[:], ALU.mult))
                        v = qk[:, t % 2, :].rearrange("p (h d) -> p h d", d=DH)
                        V.tensor_tensor(v, v, ny[:].unsqueeze(2).to_broadcast((P, 2 * HEADS, DH)),
                                        ALU.mult).then_inc(qn_rdy, 1)

                    def low_qk(t):
                        dve.wait_ge(qhi_d, t + 1)
                        V.tensor_tensor(qks[:, t % 2, :, 1, :], qk[:, t % 2, :].rearrange("p (h d) -> p h d", d=DH),
                                        qks[:, t % 2, :, 0, :], ALU.subtract).then_inc(qlo_rdy, 1)

                    for t in range(NT + 1):
                        if t < NT:
                            low_v(t)
                            head_norms(t)
                        if t:
                            low_qk(t - 1)

                    def low_p(h):
                        dve.wait_ge(phi_d, h + 1)
                        V.tensor_tensor(pl[:, h % 2], pr[:, h % 3], ph[:, h % 2], ALU.subtract).then_inc(plo_rdy, 1)

                    def normalize(h):
                        dve.wait_ge(o_ps, h + 1)
                        o = O[h % 2][:, 0:NT * (DH + 1)].rearrange("p (c d) -> p c d", d=DH + 1)
                        done(V.reciprocal(rd[:, h % 2, :], o[:, :, DH]))
                        V.tensor_tensor(O_sb[:, :, h * DH:(h + 1) * DH], o[:, :, 0:DH],
                                        rd[:, h % 2, :].unsqueeze(2).to_broadcast((P, NT, DH)),
                                        ALU.mult).then_inc(o_rdy, 1)

                    def pair(j):
                        dve.wait_ge(ot_ps, j + 1)
                        if j >= 2:
                            dve.wait_ge(wo_ps, j - 1)
                        V.tensor_copy(OT[:, j % 2, :], M6[:]).then_inc(ot_rdy, 1)

                    for h in range(HEADS):
                        low_p(h)
                        if h:
                            normalize(h - 1)
                        if h % 2 and h >= 3:
                            pair(h // 2 - 1)
                    normalize(HEADS - 1)
                    pair(PAIRS - 1)

                    dve.wait_ge(wo_ps, PAIRS)
                    V.tensor_scalar(aT[:], M7[:], mod[:, 2:3], None, ALU.mult).then_inc(aT_rdy, 1)
                    dve.wait_ge(at_ps, 1)
                    done(V.tensor_tensor(x1[:].rearrange("p t d -> p (t d)"), M6[:],
                                         x_sb[:].rearrange("p t d -> p (t d)"), ALU.add))
                    layernorm(x1, x1_rdy)
                    dve.wait_ge(x2_ps, 1)
                    V.tensor_scalar(hT[:], M7[:], mod[:, 4:5], mod[:, 3:4], ALU.mult, ALU.add).then_inc(h2_rdy, 1)

                    dve.wait_ge(lg_ex, 1)
                    done(V.tensor_scalar(ex[:], ex[:], 1.0, None, ALU.add))
                    done(V.reciprocal(sco[:], ex[:]))
                    done(V.tensor_tensor(scb[:], sco[:], eb_sb[:].unsqueeze(1).to_broadcast((P, NT, E)), ALU.add))
                    v = scb[:].rearrange("p t (g a c) -> p (t g) a c", a=2, c=2)
                    w = g1[:].rearrange("p t g w -> p (t g) w")
                    done(V.tensor_tensor(w[:, :, 0:2], v[:, :, :, 0], v[:, :, :, 1], ALU.max))
                    done(V.tensor_tensor(w[:, :, 2:4], v[:, :, :, 0], v[:, :, :, 1], ALU.min))
                    f = gs[:].rearrange("p t g -> p (t g)")
                    f2 = gm[:].rearrange("p t g -> p (t g)")
                    done(V.tensor_tensor(f, w[:, :, 2], w[:, :, 3], ALU.max))
                    done(V.tensor_tensor(f2, w[:, :, 0], w[:, :, 1], ALU.min))
                    done(V.tensor_tensor(f, f, f2, ALU.max))
                    done(V.tensor_tensor(f2, w[:, :, 0], w[:, :, 1], ALU.max))
                    done(V.tensor_tensor(f, f, f2, ALU.add))
                    own = gs[:].unsqueeze(3).to_broadcast((P, NT, NG, NG))
                    other = gs[:].unsqueeze(2).to_broadcast((P, NT, NG, NG))
                    done(V.tensor_tensor(bt[:], other, own, ALU.is_gt))
                    done(V.tensor_tensor(bt2[:], other, own, ALU.is_equal))
                    done(V.tensor_tensor(bt2[:], bt2[:], lt[:].unsqueeze(1).to_broadcast((P, NT, NG, NG)), ALU.mult))
                    done(V.tensor_tensor(bt[:], bt[:], bt2[:], ALU.add))
                    done(V.tensor_reduce(gm[:], bt[:], AX_X, ALU.add))
                    done(V.tensor_scalar(gm[:], gm[:], float(TOPG), None, ALU.is_lt))
                    done(V.tensor_tensor(scb[:].rearrange("p t (g c) -> p (t g) c", c=EG),
                                         scb[:].rearrange("p t (g c) -> p (t g) c", c=EG),
                                         gm[:].rearrange("p t g -> p (t g)").unsqueeze(2)
                                         .to_broadcast((P, NT * NG, EG)), ALU.mult))
                    for t in range(NT):
                        last = V.max(top[:, t, :], scb[:, t, :])
                    done(last)
                    fourth = top[:, :, TOPK - 1:TOPK].to_broadcast((P, NT, E))
                    done(V.tensor_tensor(sel[:], scb[:], fourth, ALU.is_gt))
                    done(V.tensor_tensor(eq[:, 0, :, E:2 * E], scb[:], fourth, ALU.is_equal))
                    done(V.tensor_reduce(need[:], sel[:], AX_X, ALU.add))
                    done(V.tensor_scalar(need[:], need[:], -1.0, float(TOPK), ALU.mult, ALU.add))
                    done(V.tensor_copy(cmb[:], eq[:, 0, :, E:2 * E]))
                    for i, s in enumerate((1, 2, 4, 8)):
                        done(V.tensor_tensor(eq[:, (i + 1) % 2, :, E:2 * E], eq[:, i % 2, :, E:2 * E],
                                             eq[:, i % 2, :, E - s:2 * E - s], ALU.add))
                    done(V.tensor_tensor(eq[:, 0, :, E:2 * E], eq[:, 0, :, E:2 * E],
                                         need[:].unsqueeze(2).to_broadcast((P, NT, E)), ALU.is_le))
                    done(V.tensor_tensor(cmb[:], cmb[:], eq[:, 0, :, E:2 * E], ALU.mult))
                    done(V.tensor_tensor(sel[:], sel[:], cmb[:], ALU.add))
                    done(V.tensor_tensor(cmb[:], sel[:], sco[:], ALU.mult))
                    done(V.tensor_reduce(need[:], cmb[:], AX_X, ALU.add))
                    done(V.tensor_scalar(need[:], need[:], 1e-20, None, ALU.add))
                    done(V.reciprocal(need[:], need[:]))
                    done(V.tensor_scalar(need[:], need[:], ROUTE_SCALE, None, ALU.mult))
                    done(V.tensor_tensor(cmb[:], cmb[:], need[:].unsqueeze(2).to_broadcast((P, NT, E)), ALU.mult))
                    done(V.tensor_copy(cs[:, :, 0, :], cmb[:]))
                    V.tensor_tensor(cs[:, :, 1, :], cmb[:], cs[:, :, 0, :], ALU.subtract).then_inc(cs_rdy, 1)
                    dve.wait_ge(ct_ps, 1)
                    V.tensor_copy(cT_sb[0:2 * E, :], M6[0:2 * E, :].bitcast(F16)[:, 0:SEQ]).then_inc(cT_rdy, 1)

                    for j in range(NJ):
                        G, U = S[j % 2][:, 0, :], S[j % 2][:, 1, :]
                        dve.wait_ge(th_d, j + 1)
                        if j:
                            dve.wait_ge(hj_rdy, j)
                        if j >= 2:
                            dve.wait_ge(dn_ps, j - 1)
                        done(V.scalar_tensor_tensor(ga_[:, 0, :], th[:, j % 2, :], 1.0, G, ALU.add, ALU.mult))
                        if j == 0:
                            V.scalar_tensor_tensor(hj[:, 0, :], ga_[:, 0, :], 0.5, U,
                                                   ALU.mult, ALU.mult).then_inc(hj_rdy, 1)
                        else:
                            done(V.scalar_tensor_tensor(ga_[:, 1, :], ga_[:, 0, :], 0.5, U, ALU.mult, ALU.mult))
                            dve.wait_ge(cb_ps, j)
                            V.tensor_tensor(hj[:, j % 2, :], ga_[:, 1, :], O[j % 2][:], ALU.mult).then_inc(hj_rdy, 1)
                    dve.wait_ge(dn_ps, NJ)
                    V.tensor_scalar(aT[:], M7[:], mod[:, 5:6], None, ALU.mult).then_inc(yT_rdy, 1)
                    dve.wait_ge(y_ps, 1)
                    V.tensor_tensor(o_sb[:].rearrange("p t d -> p (t d)"), M6[:],
                                    x1[:].rearrange("p t d -> p (t d)"), ALU.add).then_inc(out_rdy, 1)

            for s in sems:
                nc.sync.sem_clear(s)
            nc.all_engine_barrier()


def kernel(**inputs):
    import numpy as _np
    import concourse.bacc as _bacc
    from concourse import mybir as _mybir
    from concourse.bass_utils import run_bass_kernel_spmd as _run

    a = {k.removeprefix("L0_"): _np.asarray(v) for k, v in inputs.items()}
    cat = _np.concatenate
    arrays = {
        "x": a["attn_tokens"],
        "wqkv": cat([a["attn_Wq"], a["attn_Wkv"]], axis=1),
        "wo": a["attn_Wo"].reshape(PAIRS, P, P).transpose(1, 0, 2),
        "wg": cat([a["ffn_gate_w"].reshape(-1, P), a["ffn_sh_gate_w"]]).reshape(NJ, P, P).transpose(2, 0, 1),
        "wu": cat([a["ffn_up_w"].reshape(-1, P), a["ffn_sh_up_w"]]).reshape(NJ, P, P).transpose(2, 0, 1),
        "wd": cat([a["ffn_down_w"].transpose(0, 2, 1).reshape(-1, P), a["ffn_sh_down_w"].T])
        .reshape(NJ, P, P).transpose(1, 0, 2),
        "wr": a["ffn_router_weight"].T,
        "gq": a["attn_q_gamma"].reshape(1, HD),
        "gk": a["attn_k_gamma"].reshape(1, HD),
        "nw": a["attn_norm_w"].reshape(P, 1),
        "ebias": a["ffn_e_bias"].reshape(1, E),
        "cT": a["c"].T,
        "wmod": a["wmod"].reshape(P, 6, P),
    }
    nc = _bacc.Bacc("TRN2", target_bir_lowering=False, num_devices=1)
    given, args = {}, []
    for name, v in arrays.items():
        v = _np.ascontiguousarray(v)
        given[f"in_{name}"] = v
        args.append(nc.dram_tensor(f"in_{name}", v.shape, _mybir.dt.from_np(v.dtype), kind="ExternalInput").ap())
    args.append(nc.dram_tensor("out_0", (NB, SEQ, P), F32, kind="ExternalOutput").ap())
    block_kernel(nc, *args)
    r = _run(nc, [given], core_ids=[0])
    return r.results[0]["out_0"]
```

```python
from contextlib import ExitStack

import concourse.bass as bass
from concourse import mybir

F32 = mybir.dt.float32
F16 = mybir.dt.float16
I32 = mybir.dt.int32
ALU = mybir.AluOpType
ACT = mybir.ActivationFunctionType
AX_X = mybir.AxisListType.X

P = 128
NB = 8
SEQ = 512
NT = SEQ // P
HEADS = 16
DH = 64
HD = HEADS * DH
GH = 4
GROUPS = HEADS // GH
GW = GH * DH
PAIRS = HEADS // 2
E = 16
NG = 4
EG = E // NG
TOPK = 4
TOPG = 2
I_MOE = 64
NJ = E * I_MOE // P + 1
SOFTCLAMP = 50.0
QSCALE = DH ** 0.5
LN_EPS = 1e-5
RMS_EPS = 1.1920928955078125e-07
NORM_MIN = 1e-12
ROUTE_SCALE = 2.5
GATE_MIN = 0.25
FFN0 = 6
VEC_STEPS = 180
MAGIC = 1597463007.0


def block_kernel(nc, x, wqkv, wo, wg, wu, wd, wr, gq, gk, nw, ebias, cT, wmod, out):
    ctx = ExitStack()
    with ctx:
        def sb(name, shape, dt=F32):
            return ctx.enter_context(nc.sbuf_tensor(name, shape, dt))

        def ps(name, shape, dt=F32):
            return ctx.enter_context(nc.psum_tensor(name, shape, dt))

        sems = []

        def sem(name):
            s = ctx.enter_context(nc.semaphore(name))
            sems.append(s)
            return s

        wqkv_sb = sb("wqkv_sb", [P, GROUPS, 3 * GW])
        wo_sb = sb("wo_sb", [P, PAIRS, P])
        wg_sb = sb("wg_sb", [P, NJ, P])
        wu_sb = sb("wu_sb", [P, NJ, P])
        wd_sb = sb("wd_sb", [P, NJ, P])
        wr_sb = sb("wr_sb", [P, E])
        gam = sb("gam", [P, HD])
        nw_sb = sb("nw_sb", [P, 1])
        eb_sb = sb("eb_sb", [P, E])
        c_sb = sb("c_sb", [P, NB])
        cth = sb("cth", [P, NB])
        modT = sb("modT", [P, 6, NB])
        mtmp = sb("mtmp", [P, 2, NB])
        ident = sb("ident", [P, P])
        ident16 = sb("ident16", [P, P], F16)
        ones = sb("ones", [P, 1])
        expand = sb("expand", [P, NJ - 1, P], F16)
        lt = sb("lt", [P, NG, NG])

        NW = NT * 2 * GH
        x_in = sb("x_in", [P, NT, P])
        modA = sb("modA", [P, 6])
        modC = sb("modC", [P, 6])
        st = sb("st", [P, NT, 6])
        mv = sb("mv", [P, NT, 2])
        xh = sb("xh", [P, NT, P])
        hQ = sb("hQ", [P, SEQ])
        hV = sb("hV", [P, SEQ])
        sqT = xh[:].rearrange("p t d -> p (t d)")
        aux = sb("aux", [P, SEQ])
        r1 = sb("r1", [P, NT])
        hn = sb("hn", [P, NW])
        rQ = sb("rQ", [P, NT])
        rV = sb("rV", [P, NT])
        nx = sb("nx", [P, NW])
        ny = sb("ny", [P, NW])
        nt_ = sb("nt_", [P, NW])
        ss = sb("ss", [P, 2, NT, 2 * GH])
        qk = sb("qk", [P, 2, NT, 2, GW])
        sq = sb("sq", [P, 2 * GW])
        qks = sb("qks", [P, 2, 2 * GH, 2, DH], F16)
        QK = sb("QK", [P, 2, HEADS, SEQ], F16)
        KS = sb("KS", [P, HEADS, SEQ], F16)
        Vh = sb("Vh", [P, NT, HEADS, DH + 1], F16)
        Vl = sb("Vl", [P, NT, HEADS, DH], F16)
        pr = sb("pr", [P, 2, NT, SEQ])
        ph = sb("ph", [P, 2, NT, SEQ], F16)
        pl = sb("pl", [P, 2, NT, SEQ], F16)
        rd = sb("rd", [P, NT])
        O_sb = sb("O_sb", [P, NT, 2, 2, DH])
        OT = sb("OT", [P, PAIRS, SEQ])
        aT = sb("aT", [P, SEQ])
        x1 = sb("x1", [P, NT, P])
        h2T = sb("h2T", [P, SEQ])
        ex = sb("ex", [P, NT, E])
        sco = sb("sco", [P, NT, E])
        scb = sb("scb", [P, NT, E])
        g1 = sb("g1", [P, NT, NG, 4])
        gs = sb("gs", [P, NT, NG])
        bt = sb("bt", [P, NT, NG, NG])
        bt2 = sb("bt2", [P, NT, NG, NG])
        gm = sb("gm", [P, NT, NG])
        top = sb("top", [P, NT, 8])
        sel = sb("sel", [P, NT, E])
        eq = sb("eq", [P, 2, NT, 2 * E])
        need = sb("need", [P, NT])
        cmb = sb("cmb", [P, NT, E])
        cs = sb("cs", [P, NT, 2, E], F16)
        cT_sb = sb("cT_sb", [P, SEQ], F16)
        th = sb("th", [P, SEQ // 2])
        ga_ = sb("ga_", [P, SEQ // 2])
        hb = sb("hb", [P, SEQ])
        hj = sb("hj", [P, 2, SEQ])
        o_sb = sb("o_sb", [P, NT, P])
        gq_sb = pr[:, 0].rearrange("p a q -> p (a q)")[:, 0:HD]
        spread0 = pr[:, 1].rearrange("p a q -> p (a q)")[:, 0:HD]

        wmod_sb = pr[:, 1].rearrange("p a q -> p (a q)")[:, HD:HD + 6 * P].rearrange("p (j d) -> p j d", j=6)

        S = [ps(f"S{i}", [P, 2, SEQ]) for i in range(2)]
        O = ps("O", [P, SEQ])
        ACC = ps("ACC", [P, SEQ])
        M6 = ps("M6", [P, SEQ])
        M7 = ps("M7", [P, SEQ])
        T16 = M6[:, :].bitcast(F16).rearrange("p (h t) -> p h t", t=P)
        C16 = M7[:, :].bitcast(F16)

        load = ctx.enter_context(nc.semaphore("load"))
        built = ctx.enter_context(nc.semaphore("built"))
        vec0 = ctx.enter_context(nc.semaphore("vec0"))
        silu_c = ctx.enter_context(nc.semaphore("silu_c"))
        modp = ctx.enter_context(nc.semaphore("modp"))
        LOADS = 13
        with nc.Block() as block:
            @block.sync
            def _(sp):
                for dst, src in ((c_sb[:], cT), (wmod_sb, wmod), (wqkv_sb[:], wqkv), (nw_sb[:], nw),
                                 (gam[:], gk.to_broadcast((P, HD))), (gq_sb, gq.to_broadcast((P, HD))),
                                 (eb_sb[:], ebias.to_broadcast((P, E))), (wo_sb[:], wo), (wr_sb[:], wr),
                                 (wg_sb[:], wg), (wu_sb[:], wu), (wd_sb[:], wd)):
                    sp.dma_start(dst, src).then_inc(load, 16)

            @block.gpsimd
            def _(pool):
                pool.memset(ident[:], 0.0).then_inc(built, 1)
                pool.memset(expand[:], 1.0).then_inc(built, 1)
                pool.memset(lt[:], 1.0).then_inc(built, 1)
                pool.memset(ones[:], 1.0).then_inc(built, 1)
                pool.memset(eq[:], 0.0).then_inc(built, 1)
                pool.memset(cT_sb[:], 0.0).then_inc(built, 1)
                pool.memset(Vh[:], 1.0).then_inc(built, 1)
                pool.wait_ge(built, 7)
                pool.affine_select(out=ident[:], in_=ident[:], compare_op=ALU.not_equal, fill=1.0,
                                   base=0, pattern=[[-1, P]], channel_multiplier=1).then_inc(built, 1)
                pool.memset(spread0, 0.0).then_inc(built, 1)
                pool.wait_ge(built, 9)
                for r in range(2):
                    v = spread0.rearrange("p (e i) -> p e i", i=I_MOE)
                    pool.affine_select(out=v, in_=v, compare_op=ALU.not_equal, fill=1.0,
                                       base=-E * r, pattern=[[-1, E], [0, I_MOE]],
                                       channel_multiplier=1).then_inc(built, 1)
                    pool.wait_ge(built, 10 + r)
                pool.affine_select(out=lt[:], in_=lt[:], compare_op=ALU.is_ge, fill=0.0,
                                   base=-1, pattern=[[1, NG], [-1, NG]],
                                   channel_multiplier=0).then_inc(built, 1)

            @block.vector
            def _(dve):
                n = [0]

                def done(ins):
                    n[0] += 1
                    ins.then_inc(vec0, 1)
                    dve.wait_ge(vec0, n[0])

                dve.wait_ge(built, 12)
                done(nc.vector.tensor_copy(ident16[:], ident[:]))
                done(nc.vector.tensor_copy(expand[:].rearrange("p j f -> p (j f)"), spread0))
                dve.wait_ge(load, 16 * (LOADS - 1))
                done(nc.vector.tensor_scalar(wqkv_sb[:], wqkv_sb[:], nw_sb[:], None, ALU.mult))
                done(nc.vector.tensor_scalar(gq_sb, gq_sb, 1.0, None, ALU.add))
                done(nc.vector.scalar_tensor_tensor(gam[:], gam[:], 1.0, gq_sb, ALU.add, ALU.mult))
                dve.wait_ge(silu_c, 1)
                done(nc.vector.scalar_tensor_tensor(cth[:], cth[:], 1.0, c_sb[:], ALU.add, ALU.mult))
                nc.vector.tensor_scalar(cth[:], cth[:], 0.5, None, ALU.mult).then_inc(silu_c, 1)
                dve.wait_ge(modp, 1)
                m = M7[:, 0:6 * NB].rearrange("p (j b) -> p j b", j=6)
                done(nc.vector.tensor_copy(modT[:], m))
                for j in (1, 4):
                    done(nc.vector.tensor_scalar(modT[:, j, :], modT[:, j, :], 1.0, None, ALU.add))
                for j in (2, 5):
                    g = modT[:, j, :]
                    done(nc.vector.tensor_scalar(mtmp[:, 0, :], g, 0.0, 2.0, ALU.is_ge, ALU.mult))
                    done(nc.vector.tensor_scalar(mtmp[:, 0, :], mtmp[:, 0, :], -1.0, None, ALU.add))
                    done(nc.vector.tensor_tensor(mtmp[:, 1, :], g, mtmp[:, 0, :], ALU.mult))
                    done(nc.vector.tensor_scalar(mtmp[:, 1, :], mtmp[:, 1, :], GATE_MIN, None, ALU.max))
                    done(nc.vector.tensor_tensor(g, mtmp[:, 1, :], mtmp[:, 0, :], ALU.mult))

            @block.scalar
            def _(act):
                act.wait_ge(load, 16 * (LOADS - 1))
                nc.scalar.activation(cth[:], c_sb[:], ACT.Tanh, scale=0.5).then_inc(silu_c, 1)

            @block.tensor
            def _(pe):
                pe.wait_ge(silu_c, 2)
                pe.wait_ge(load, 16 * (LOADS - 1))
                for j in range(6):
                    last = nc.tensor.matmul(M7[:, j * NB:(j + 1) * NB], wmod_sb[:, j, :], cth[:],
                                            start=True, stop=True)
                last.then_inc(modp, 1)

        x_ld = sem("x_ld")
        xr_ld = sem("xr_ld")
        k_swap = [sem(f"k_swap{g}") for g in range(GROUPS)]
        stored = sem("stored")
        vec = sem("vec")
        xh_rdy = sem("xh_rdy")
        hQ_rdy = sem("hQ_rdy")
        sq_rdy = sem("sq_rdy")
        r1_rdy = sem("r1_rdy")
        hV_rdy = sem("hV_rdy")
        v_evac = sem("v_evac")
        ss_rdy = sem("ss_rdy")
        qn_rdy = sem("qn_rdy")
        qlo_rdy = sem("qlo_rdy")
        plo_rdy = sem("plo_rdy")
        o_rdy = sem("o_rdy")
        aT_rdy = sem("aT_rdy")
        x1_sum = sem("x1_sum")
        x1_rdy = sem("x1_rdy")
        h2_rdy = sem("h2_rdy")
        cs_rdy = sem("cs_rdy")
        cT_rdy = sem("cT_rdy")
        gu_rd = sem("gu_rd")
        hj_rdy = sem("hj_rdy")
        yT_rdy = sem("yT_rdy")
        out_rdy = sem("out_rdy")
        xT_ps = sem("xT_ps")
        ms_ps = sem("ms_ps")
        qk_ps, v_ps = sem("qk_ps"), sem("v_ps")
        t_ps = sem("t_ps")
        s_ps = sem("s_ps")
        o_ps = sem("o_ps")
        ot_ps = sem("ot_ps")
        wo_ps = sem("wo_ps")
        at_ps = sem("at_ps")
        x2_ps = sem("x2_ps")
        lg_ps = sem("lg_ps")
        gu_ps = sem("gu_ps")
        ct_ps = sem("ct_ps")
        cb_ps = sem("cb_ps")
        dn_ps = sem("dn_ps")
        y_ps = sem("y_ps")
        qk_ev = sem("qk_ev")
        v_ev = sem("v_ev")
        t_ev = sem("t_ev")
        tanh_d = sem("tanh_d")
        exp_d = sem("exp_d")
        ot_rdy = sem("ot_rdy")
        lg_ex = sem("lg_ex")
        th_d = sem("th_d")
        sq_d = sem("sq_d")
        kg_d = sem("kg_d")
        qhi_d = sem("qhi_d")
        phi_d = sem("phi_d")

        LAST = NB * HEADS

        held = sem("held")

        def live(b, h, ahead=0):
            return not isinstance(b, int) or 0 <= HEADS * b + h + ahead < LAST

        def batch(b):
            return not isinstance(b, int) or 0 <= b < NB

        def first(b, n=1):
            return isinstance(b, int) and b < n

        def hold(eng, s, value):
            eng.wait_ge(s, value)
            if not isinstance(value, int):
                eng.sem_inc(held, 1)

        def run(eng, slot, segment=None):
            for b in (-1, 0):
                for h in range(HEADS):
                    slot(b, h)
            if segment:
                segment(1)
            with eng.Fori(1, NB - 1) as b:
                for h in range(HEADS):
                    slot(b, h)
            if segment:
                segment(NB - 1)
            for b in (NB - 1, NB):
                for h in range(HEADS):
                    slot(b, h)

        with nc.Block() as block:
            @block.sync
            def _(sp):
                def slot(b, h):
                    if h == 0 and batch(b + 1):
                        if not first(b + 1):
                            sp.wait_ge(xh_rdy, (b + 1) * NT)
                        sp.dma_start(x_in[:], x[b + 1].rearrange("(t p) d -> p t d", p=P)).then_inc(x_ld, 16)
                    if h == 0 and batch(b - 1):
                        if not first(b - 1):
                            sp.wait_ge(out_rdy, b - 1)
                        sp.dma_start(x1[:], x[b - 1].rearrange("(t p) d -> p t d", p=P)).then_inc(xr_ld, 16)
                    if h % GH == 1 and live(b, h, 3):
                        g = (h + 3) % HEADS // GH
                        hs = slice(GH * g, GH * g + GH)
                        sp.wait_ge(t_ev, HEADS * b + h + 7)
                        sp.dma_start(KS[DH:P, hs, :], QK[0:DH, 1, hs, :]).then_inc(k_swap[g], 16)
                        sp.dma_start(KS[0:DH, hs, :], QK[DH:P, 1, hs, :]).then_inc(k_swap[g], 16)
                    if h == HEADS - 1 and batch(b - 1):
                        sp.wait_ge(out_rdy, b)
                        sp.dma_start(out[b - 1].rearrange("(t p) d -> p t d", p=P), o_sb[:]).then_inc(stored, 16)
                run(sp, slot)
                sp.wait_ge(stored, 16 * NB)

            @block.gpsimd
            def _(pool):
                def slot(b, h):
                    i, s = h % GH, HEADS * b + h
                    if live(b, h, 11):
                        par, g, t = ((h + 11) // GH) % 2, (h + 11) % HEADS // GH, (h + 11) % NT
                        a = s + 11
                        hold(pool, qk_ev, a + 1)
                        if not isinstance(b, int) or a >= 1:
                            hold(pool, ss_rdy, a)
                        nc.gpsimd.tensor_tensor(sq[:], qk[:, par, t].rearrange("p r n -> p (r n)"),
                                                qk[:, par, t].rearrange("p r n -> p (r n)"),
                                                ALU.mult).then_inc(sq_d, 1)
                        pool.wait_ge(sq_d, a + 1)
                        nc.gpsimd.tensor_tensor(qk[:, par, t, 1], qk[:, par, t, 1], gam[:, GW * g:GW * g + GW],
                                                ALU.mult).then_inc(kg_d, 1)
                    if live(b, h):
                        hold(pool, exp_d, 2 * s + 2)
                        if not isinstance(b, int) or s >= 2:
                            hold(pool, o_ps, s - 1)
                        nc.gpsimd.tensor_scalar(ph[:, h % 2].rearrange("p a q -> p (a q)"),
                                                pr[:, h % 2].rearrange("p a q -> p (a q)"),
                                                1.0, 0.0, ALU.mult, ALU.add).then_inc(phi_d, 1)
                    if live(b, h, 8):
                        par = ((h + 8) // GH) % 2
                        hold(pool, qn_rdy, s + 8 + 1)
                        if live(b, h, 6):
                            hold(pool, t_ps, s + 6 + 1)
                        nc.gpsimd.tensor_scalar(qks[:, h % 2, :, 0, :],
                                                qk[:, par, i].rearrange("p r (h d) -> p (r h) d", d=DH),
                                                1.0, 0.0, ALU.mult, ALU.add).then_inc(qhi_d, 1)
                run(pool, slot)

            @block.scalar
            def _(act):
                def tanh(b, h, u):
                    if live(b, h, 1):
                        s, k = HEADS * b + h + 1, (h + 1) % 2
                        act.wait_ge(s_ps, 2 * s + u + 1)
                        if u == 0 and (not isinstance(b, int) or s >= 2):
                            act.wait_ge(plo_rdy, s - 1)
                        nc.scalar.activation(pr[:, k, 2 * u:2 * u + 2, :], S[u][:], ACT.Tanh,
                                             scale=QSCALE * QSCALE / SOFTCLAMP).then_inc(tanh_d, 1)

                def exponential(b, h, u):
                    if live(b, h):
                        s = HEADS * b + h
                        act.wait_ge(tanh_d, 2 * s + u + 1)
                        half = pr[:, h % 2, 2 * u:2 * u + 2, :]
                        nc.scalar.activation(half, half, ACT.Exp, scale=SOFTCLAMP * DH ** -0.5).then_inc(exp_d, 1)

                def slot(b, h):
                    i, s, c = h % GH, HEADS * b + h, b - 1
                    tile = h - FFN0
                    if live(b, h, 6):
                        g, t = (h + 6) % HEADS // GH, (h + 6) % NT
                        act.wait_ge(t_ps, s + 6 + 1)
                        nc.scalar.activation(QK[:, :, GH * g:GH * g + GH, t * P:(t + 1) * P],
                                             T16.rearrange("p (r h) t -> p r h t", r=2), ACT.Copy).then_inc(t_ev, 1)
                    gate(b, tile, 0)
                    exponential(b, h, 1)
                    if live(b, h, 12):
                        par, a = ((h + 12) // GH) % 2, s + 12
                        act.wait_ge(qk_ps, a + 1)
                        if h == 4:
                            act.wait_ge(hQ_rdy, b + 2)
                        if not isinstance(b, int) or a >= 8:
                            act.wait_ge(qlo_rdy, a - 8 + 1)
                        nc.scalar.activation(qk[:, par, i].rearrange("p r n -> p (r n)"), M6[:], ACT.Copy,
                                             scale=rQ[:, i:i + 1]).then_inc(qk_ev, 1)
                    gate(b, tile, 1)
                    tanh(b, h, 0)
                    if live(b, h, 8):
                        g, a = (h + 8) % HEADS // GH, s + 8
                        act.wait_ge(v_ps, a + 1)
                        if h == 8:
                            act.wait_ge(hV_rdy, b + 2)
                        nc.scalar.activation(Vh[:, i, GH * g:GH * g + GH, 0:DH],
                                             M6[:, 0:GW].rearrange("p (h d) -> p h d", d=DH), ACT.Copy,
                                             scale=rV[:, i:i + 1]).then_inc(v_ev, 1)
                    tanh(b, h, 1)
                    j = (h - 3) // 2
                    if h % 2 and live(b, h, -3):
                        n = PAIRS * b + j
                        act.wait_ge(ot_ps, n + 1)
                        if j == 0 and not first(b, 1):
                            act.wait_ge(wo_ps, b)
                        nc.scalar.activation(OT[:, j % PAIRS, :], M7[:], ACT.Copy).then_inc(ot_rdy, 1)
                    if batch(c) and h == 4:
                        act.wait_ge(lg_ps, b)
                        nc.scalar.activation(ex[:].rearrange("p t e -> p (t e)"), M7[:, 0:NT * E], ACT.Exp,
                                             scale=-1.0).then_inc(lg_ex, 1)
                    if h + 1 < HEADS:
                        exponential(b, h + 1, 0)
                    else:
                        exponential(b + 1, 0, 0)

                def gate(b, tile, a):
                    if batch(b - 1) and 0 <= tile < NJ:
                        n = 2 * NJ * (b - 1) + 2 * tile + a
                        act.wait_ge(gu_ps, n + 1)
                        if not isinstance(b, int) or n:
                            act.wait_ge(gu_rd, n)
                        nc.scalar.activation(th[:], M7[:, 0:SEQ // 2], ACT.Tanh, scale=0.5).then_inc(th_d, 1)
                run(act, slot)

            @block.tensor
            def _(pe):
                mm = nc.tensor.matmul

                def transpose4(dst, src):
                    for t in range(NT):
                        last = nc.tensor.transpose(dst[:, t * P:(t + 1) * P], src(t), ident[:])
                    return last

                def scores(b, h, u):
                    s, k = HEADS * b + h + 1, (h + 1) % HEADS
                    if k % GH == 0 and u == 0:
                        kb = b if h + 1 < HEADS else b + 1
                        pe.wait_ge(k_swap[k // GH], 32 * kb + 32)
                    if not isinstance(b, int) or s >= 1:
                        pe.wait_ge(tanh_d, 2 * (s - 1) + u + 1)
                    for a in range(2):
                        ks = slice((2 * u + a) * P, (2 * u + a + 1) * P)
                        mm(S[u][:, a, :], QK[:, 1, k, ks], QK[:, 0, k, :], start=True, stop=False)
                        last = mm(S[u][:, a, :], KS[:, k, ks], QK[:, 0, k, :], start=False, stop=True)
                    last.then_inc(s_ps, 1)

                def values(b, h):
                    s, k = HEADS * b + h - 1, (h - 1) % HEADS
                    pe.wait_ge(plo_rdy, s + 1)
                    pe.wait_ge(v_evac, s - k % GH + GH)
                    if not isinstance(b, int) or s >= 1:
                        pe.wait_ge(o_rdy, s)
                    for c in range(NT):
                        o = O[:, c * (DH + 1):(c + 1) * (DH + 1)]
                        qs = slice(c * P, (c + 1) * P)
                        for t in range(NT):
                            mm(o, ph[:, k % 2, t, qs], Vh[:, t, k, :], start=(t == 0), stop=False)
                            mm(o[:, 0:DH], ph[:, k % 2, t, qs], Vl[:, t, k, :], start=False, stop=False)
                            last = mm(o, pl[:, k % 2, t, qs], Vh[:, t, k, :], start=False, stop=(t == NT - 1))
                    last.then_inc(o_ps, 1)

                def layernorm_x(b, h):
                    if not batch(b + 1):
                        return
                    if h == 2:
                        pe.wait_ge(xh_rdy, NT * (b + 2))
                        if live(b, h, -3):
                            pe.wait_ge(ot_rdy, PAIRS * b)
                        transpose4(M7, lambda t: xh[:, t, :]).then_inc(xT_ps, 1)
                        pe.wait_ge(sq_rdy, b + 2)
                        for t in range(NT):
                            last = mm(M7[:, t:t + 1], sqT[:, t * P:(t + 1) * P], ones[:], start=True, stop=True)
                        last.then_inc(ms_ps, 1)

                def slot(b, h):
                    i, s, c = h % GH, HEADS * b + h, b - 1
                    tile = h - FFN0
                    ffn = batch(c) and 0 <= tile < NJ
                    if live(b, h, 6):
                        pe.wait_ge(qlo_rdy, s + 6 + 1)
                        if live(b, h, 7):
                            pe.wait_ge(v_evac, s + 8)
                        elif live(b, h, 5):
                            pe.wait_ge(t_ev, s + 6)
                        for n in range(2 * GH):
                            last = nc.tensor.transpose(T16[:, n, :],
                                                       qks[:, h % 2, n].rearrange("p a d -> p (a d)"), ident16[:])
                        last.then_inc(t_ps, 1)
                    layernorm_x(b, h)
                    if ffn:
                        gate_up(b, tile, 0)
                    if live(b, h, 1):
                        scores(b, h, 0)
                    if live(b, h, 12):
                        g = (h + 12) % HEADS // GH
                        if h == 4:
                            pe.wait_ge(hQ_rdy, b + 2)
                        if live(b, h, 6):
                            pe.wait_ge(t_ev, s + 6 + 1)
                        elif live(b, h, 7):
                            pe.wait_ge(v_evac, s + 8)
                        elif live(b, h, 11):
                            pe.wait_ge(qk_ev, s + 12)
                        mm(M6[:], hQ[:, i * P:(i + 1) * P], wqkv_sb[:, g, 0:2 * GW], start=True,
                           stop=True).then_inc(qk_ps, 1)
                    if ffn:
                        gate_up(b, tile, 1)
                    if live(b, h, 1):
                        scores(b, h, 1)
                    if live(b, h, 8):
                        g = (h + 8) % HEADS // GH
                        if h == 8:
                            pe.wait_ge(hV_rdy, b + 2)
                        if live(b, h, 12):
                            pe.wait_ge(qk_ev, s + 13)
                        elif live(b, h, 6):
                            pe.wait_ge(t_ev, s + 7)
                        mm(M6[:, 0:GW], hV[:, i * P:(i + 1) * P], wqkv_sb[:, g, 2 * GW:3 * GW], start=True,
                           stop=True).then_inc(v_ps, 1)
                    if ffn and tile:
                        spread(b, tile)
                    if live(b, h, -1):
                        values(b, h)
                    if h % 2 and live(b, h, -3):
                        n, pj = PAIRS * b + (h - 3) // 2, ((h - 3) // 2) % 2
                        pe.wait_ge(o_rdy, 2 * n + 2)
                        before_pair(b, h)
                        transpose4(M7, lambda t: O_sb[:, t, pj].rearrange("p e d -> p (e d)")).then_inc(ot_ps, 1)
                    finish(b, h)

                def before_pair(b, h):
                    c = b - 1
                    if h == 1:
                        pe.wait_ge(ot_rdy, PAIRS * b - 1)
                    elif h == 3:
                        if batch(b + 1):
                            pe.wait_ge(r1_rdy, b + 2)
                        if batch(c):
                            pe.wait_ge(x1_sum, b)
                    elif h == 5 and batch(c):
                        pe.wait_ge(lg_ex, b)
                    elif batch(c) and h < HEADS - 1:
                        if h == FFN0:
                            pe.wait_ge(gu_rd, 2 * NJ * c + 2)
                        else:
                            pe.wait_ge(hj_rdy, (NJ - 1) * c + h - FFN0)
                    elif h == HEADS - 1 and batch(c):
                        pe.wait_ge(hj_rdy, (NJ - 1) * c + NJ - 1)
                    elif h >= 5:
                        pe.wait_ge(ot_rdy, PAIRS * b + (h - 3) // 2)

                def gate_up(b, tile, a):
                    c = b - 1
                    w = NJ - 1 if tile == 0 else tile - 1
                    h = FFN0 + tile
                    n = 2 * NJ * c + 2 * tile + a
                    if a == 1:
                        pe.wait_ge(gu_rd, n)
                    elif tile == 0:
                        pe.wait_ge(ct_ps, b)
                        pe.wait_ge(cT_rdy, b)
                    else:
                        if tile == 1:
                            pe.wait_ge(gu_rd, n)
                        else:
                            pe.wait_ge(hj_rdy, (NJ - 1) * c + tile - 1)
                        if h % 2 == 0 and live(b, h, -4):
                            pe.wait_ge(ot_rdy, PAIRS * b + (h - 4) // 2 + 1)
                    q = slice(a * SEQ // 2, (a + 1) * SEQ // 2)
                    mm(M7[:, 0:SEQ // 2], wg_sb[:, w, :], h2T[:, q], start=True, stop=True)
                    mm(M7[:, SEQ // 2:SEQ], wu_sb[:, w, :], h2T[:, q], start=True, stop=True).then_inc(gu_ps, 1)

                def spread(b, tile):
                    c = b - 1
                    pe.wait_ge(gu_rd, 2 * NJ * c + 2 * tile + 2)
                    mm(M7[:], expand[:, tile - 1, :], cT_sb[:], start=True, stop=True).then_inc(cb_ps, 1)

                def finish(b, h):
                    c = b - 1
                    if not batch(c):
                        return
                    if h in (1, 2):
                        pe.wait_ge(ot_rdy, PAIRS * b - 1 if h == 1 else PAIRS * b)
                        for j in range(4 * h - 4, 4 * h):
                            last = mm(ACC[:], wo_sb[:, j, :], OT[:, j, :], start=(j == 0), stop=(j == PAIRS - 1))
                        if h == 2:
                            last.then_inc(wo_ps, 1)
                            pe.wait_ge(aT_rdy, b)
                            if batch(b + 1):
                                pe.wait_ge(r1_rdy, b + 2)
                            transpose4(M7, lambda t: aT[:, t * P:(t + 1) * P]).then_inc(at_ps, 1)
                    if h == 3:
                        pe.wait_ge(x1_rdy, NT * b)
                        if live(b, h, -3):
                            pe.wait_ge(ot_rdy, PAIRS * b + 1)
                        transpose4(M7, lambda t: xh[:, t, :]).then_inc(x2_ps, 1)
                    if h == 4:
                        pe.wait_ge(h2_rdy, b)
                        for t in range(NT):
                            last = mm(M7[:, t * E:(t + 1) * E], h2T[:, t * P:(t + 1) * P], wr_sb[:],
                                      start=True, stop=True)
                        last.then_inc(lg_ps, 1)
                    if h == 5:
                        pe.wait_ge(cs_rdy, b)
                        if live(b, h, -3):
                            pe.wait_ge(ot_rdy, PAIRS * b + 2)
                        for t in range(NT):
                            last = nc.tensor.transpose(C16[0:2 * E, t * P:(t + 1) * P],
                                                       cs[:, t].rearrange("p a e -> p (a e)"), ident16[:])
                        last.then_inc(ct_ps, 1)
                    tile = h - FFN0 - 1
                    if 0 <= tile < NJ:
                        w = NJ - 1 if tile == 0 else tile - 1
                        if tile:
                            pe.wait_ge(hj_rdy, (NJ - 1) * c + tile)
                        else:
                            pe.wait_ge(gu_rd, 2 * NJ * c + 2)
                        mm(ACC[:], wd_sb[:, w, :], hj[:, tile % 2, :], start=(tile == 0),
                           stop=(tile == NJ - 1)).then_inc(dn_ps, 1)
                    if h == HEADS - 1:
                        pe.wait_ge(yT_rdy, b)
                        if live(b, h, -3):
                            pe.wait_ge(ot_rdy, PAIRS * b + 7)
                        transpose4(M7, lambda t: aT[:, t * P:(t + 1) * P]).then_inc(y_ps, 1)

                run(pe, slot)

            @block.vector
            def _(dve):
                V = nc.vector
                at = [0, 0, None]

                def done(ins, alone=False):
                    at[1] += 1
                    ins.then_inc(vec, 1)
                    settle(alone)

                def settle(alone=False):
                    b = at[2]
                    value = at[0] + at[1] if b is None else (b - 1) * VEC_STEPS + (at[0] + at[1])
                    if alone:
                        hold(dve, vec, value)
                    else:
                        dve.wait_ge(vec, value)

                def segment(b):
                    if b > 1:
                        assert at[1] == VEC_STEPS, at[1]
                        at[0], at[1], at[2] = at[0] + (NB - 2) * VEC_STEPS, 0, None
                    else:
                        at[0], at[1] = at[0] + at[1], 0

                def inverse_root(width):
                    X, Y, T = nx[:, 0:width], ny[:, 0:width], nt_[:, 0:width]
                    done(V.tensor_single_scalar(T.bitcast(I32), X.bitcast(I32), 1, ALU.arith_shift_right))
                    done(V.tensor_scalar(Y.bitcast(I32), T.bitcast(I32), -1.0, MAGIC, ALU.mult, ALU.add))
                    for _ in range(3):
                        done(V.scalar_tensor_tensor(T, Y, -0.5, Y, ALU.mult, ALU.mult))
                        done(V.tensor_tensor(T, T, X, ALU.mult))
                        done(V.scalar_tensor_tensor(Y, T, 1.5, Y, ALU.add, ALU.mult))

                def layernorm(src, ready):
                    for t in range(NT):
                        V.bn_stats(st[:, t, :], src[:, t, :]).then_inc(vec, 1)
                        at[1] += 1
                    settle(alone=True)
                    for t in range(NT):
                        V.bn_aggr(mv[:, t, :], st[:, t, :]).then_inc(vec, 1)
                        at[1] += 1
                    settle()
                    done(V.tensor_scalar(nx[:, 0:NT], mv[:, :, 1], LN_EPS, None, ALU.add))
                    inverse_root(NT)
                    for t in range(NT):
                        V.tensor_scalar(xh[:, t, :], src[:, t, :], mv[:, t, 0:1], ny[:, t:t + 1],
                                        ALU.subtract, ALU.mult).then_inc(ready, 1)

                def prepare(b, h):
                    if not batch(b + 1):
                        return
                    if h == 1:
                        settle()
                        done(V.tensor_copy(modA[:], modT[:, :, bass.ds(b + 1, 1)].rearrange("p j b -> p (j b)")))
                        dve.wait_ge(x_ld, 16 * (b + 2))
                        layernorm(x_in, xh_rdy)
                    if h == 2:
                        dve.wait_ge(xT_ps, b + 2)
                        done(V.tensor_scalar(aux[:], M7[:], modA[:, 1:2], modA[:, 0:1], ALU.mult, ALU.add))
                        V.tensor_tensor(sqT[:], aux[:], aux[:], ALU.mult).then_inc(sq_rdy, 1)
                        dve.wait_ge(ms_ps, b + 2)
                        done(V.tensor_scalar(nx[:, 0:NT], M7[:, 0:NT], 1.0 / P, RMS_EPS, ALU.mult, ALU.add))
                        inverse_root(NT)
                        V.tensor_copy(r1[:], ny[:, 0:NT]).then_inc(r1_rdy, 1)
                    if h == 4:
                        dve.wait_ge(r1_rdy, b + 2)
                        if live(b, h, 11):
                            dve.wait_ge(qk_ev, HEADS * b + h + 12)
                        done(V.tensor_copy(rQ[:], r1[:]))
                        V.tensor_copy(hQ[:], aux[:]).then_inc(hQ_rdy, 1)
                    if h == 8:
                        if live(b, h, 7):
                            dve.wait_ge(v_evac, HEADS * b + h + 8)
                        dve.wait_ge(hQ_rdy, b + 2)
                        done(V.tensor_copy(hV[:], hQ[:]))
                        V.tensor_copy(rV[:], rQ[:]).then_inc(hV_rdy, 1)

                def slot(b, h):
                    at[2] = None if isinstance(b, int) else b
                    i, s, c = h % GH, HEADS * b + h, b - 1
                    tile = h - FFN0
                    ffn = batch(c) and 0 <= tile < NJ
                    prepare(b, h)
                    if ffn:
                        hidden(b, tile, 0)
                    if live(b, h, 11):
                        par, t = ((h + 11) // GH) % 2, (h + 11) % NT
                        dve.wait_ge(sq_d, s + 11 + 1)
                        V.tensor_reduce(ss[:, par, t, :], sq[:].rearrange("p (h d) -> p h d", d=DH),
                                        AX_X, ALU.add).then_inc(ss_rdy, 1)
                    if live(b, h, 8):
                        par = ((h + 8) // GH) % 2
                        if i == 0:
                            dve.wait_ge(ss_rdy, s + 8 + GH)
                            done(V.tensor_scalar(nx[:], ss[:, par].rearrange("p t n -> p (t n)"),
                                                 NORM_MIN * NORM_MIN, None, ALU.max))
                            inverse_root(NW)
                            if not isinstance(b, int) or s + 8 > 0:
                                dve.wait_ge(qn_rdy, s + 8)
                            done(V.tensor_copy(hn[:], ny[:]))
                        dve.wait_ge(kg_d, s + 8 + 1)
                        v = qk[:, par, i].rearrange("p r (h d) -> p (r h) d", d=DH)
                        V.tensor_tensor(v, v, hn[:, i * 2 * GH:(i + 1) * 2 * GH].unsqueeze(2)
                                        .to_broadcast((P, 2 * GH, DH)), ALU.mult).then_inc(qn_rdy, 1)
                    if live(b, h, 7):
                        dve.wait_ge(qhi_d, s + 8)
                        par, t = ((h + 7) // GH) % 2, (h + 7) % GH
                        V.tensor_tensor(qks[:, (h - 1) % 2, :, 1, :],
                                        qk[:, par, t].rearrange("p r (h d) -> p (r h) d", d=DH),
                                        qks[:, (h - 1) % 2, :, 0, :], ALU.subtract).then_inc(qlo_rdy, 1)
                    if ffn:
                        hidden(b, tile, 1)
                    if live(b, h, 8):
                        g = (h + 8) % HEADS // GH
                        dve.wait_ge(v_ev, s + 8 + 1)
                        V.scalar_tensor_tensor(Vl[:, i, GH * g:GH * g + GH, :],
                                               M6[:, 0:GW].rearrange("p (h d) -> p h d", d=DH), rV[:, i:i + 1],
                                               Vh[:, i, GH * g:GH * g + GH, 0:DH],
                                               ALU.mult, ALU.subtract).then_inc(v_evac, 1)
                    if ffn and tile:
                        n = NJ * c + tile
                        dve.wait_ge(cb_ps, (NJ - 1) * c + tile)
                        if not isinstance(b, int) or n >= 2:
                            dve.wait_ge(dn_ps, n - 1)
                        V.tensor_tensor(hj[:, tile % 2, :], hb[:], M7[:], ALU.mult).then_inc(hj_rdy, 1)
                    finish(b, h)
                    if live(b, h):
                        dve.wait_ge(phi_d, s + 1)
                        V.tensor_tensor(pl[:, h % 2], pr[:, h % 2], ph[:, h % 2], ALU.subtract).then_inc(plo_rdy, 1)
                    if live(b, h, -1):
                        normalize(b, h)

                def hidden(b, tile, a):
                    c = b - 1
                    n = 2 * NJ * c + 2 * tile + a
                    q = slice(a * SEQ // 2, (a + 1) * SEQ // 2)
                    dve.wait_ge(th_d, n + 1)
                    if not isinstance(b, int) or n:
                        dve.wait_ge(gu_rd, n)
                    done(V.scalar_tensor_tensor(ga_[:], th[:], 1.0, M7[:, 0:SEQ // 2], ALU.add, ALU.mult))
                    if a == 0 and tile >= 2:
                        dve.wait_ge(hj_rdy, (NJ - 1) * c + tile - 1)
                    dst = hb if tile else hj[:, 0]
                    ins = V.scalar_tensor_tensor(dst[:, q], ga_[:], 0.5, M7[:, SEQ // 2:SEQ], ALU.mult, ALU.mult)
                    ins.then_inc(gu_rd, 1)

                def normalize(b, h):
                    s, k = HEADS * b + h - 1, (h - 1) % HEADS
                    dve.wait_ge(o_ps, s + 1)
                    if not isinstance(b, int) or s:
                        dve.wait_ge(o_rdy, s)
                    if k % 2 == 0 and (not isinstance(b, int) or s >= 4):
                        dve.wait_ge(ot_ps, PAIRS * b + (h - 3) // 2)
                    o = O[:, 0:NT * (DH + 1)].rearrange("p (c d) -> p c d", d=DH + 1)
                    done(V.reciprocal(rd[:], o[:, :, DH]))
                    V.tensor_tensor(O_sb[:, :, (k // 2) % 2, k % 2, :], o[:, :, 0:DH],
                                    rd[:].unsqueeze(2).to_broadcast((P, NT, DH)), ALU.mult).then_inc(o_rdy, 1)

                def finish(b, h):
                    if not batch(b - 1):
                        return
                    c = b - 1
                    if h == 2:
                        done(V.tensor_copy(modC[:], modT[:, :, bass.ds(b - 1, 1)].rearrange("p j b -> p (j b)")))
                        dve.wait_ge(wo_ps, b)
                        V.tensor_scalar(aT[:], ACC[:], modC[:, 2:3], None, ALU.mult).then_inc(aT_rdy, 1)
                        dve.wait_ge(at_ps, b)
                        dve.wait_ge(xr_ld, 16 * b)
                        V.tensor_tensor(x1[:].rearrange("p t d -> p (t d)"), M7[:],
                                        x1[:].rearrange("p t d -> p (t d)"), ALU.add).then_inc(x1_sum, 1)
                        dve.wait_ge(x1_sum, b)
                        layernorm(x1, x1_rdy)
                    if h == 3:
                        dve.wait_ge(x2_ps, b)
                        V.tensor_scalar(h2T[:], M7[:], modC[:, 4:5], modC[:, 3:4], ALU.mult, ALU.add).then_inc(h2_rdy, 1)
                    if h == 4:
                        dve.wait_ge(lg_ex, b)
                        route()
                    if h == 5:
                        dve.wait_ge(ct_ps, b)
                        V.tensor_copy(cT_sb[0:2 * E, :], C16[0:2 * E, 0:SEQ]).then_inc(cT_rdy, 1)
                    if h == HEADS - 1:
                        dve.wait_ge(dn_ps, NJ * b)
                        V.tensor_scalar(aT[:], ACC[:], modC[:, 5:6], None, ALU.mult).then_inc(yT_rdy, 1)
                        dve.wait_ge(y_ps, b)
                        if not first(c):
                            dve.wait_ge(stored, 16 * c)
                        V.tensor_tensor(o_sb[:].rearrange("p t d -> p (t d)"), M7[:],
                                        x1[:].rearrange("p t d -> p (t d)"), ALU.add).then_inc(out_rdy, 1)

                def route():
                    done(V.tensor_scalar(ex[:], ex[:], 1.0, None, ALU.add))
                    done(V.reciprocal(sco[:], ex[:]))
                    done(V.tensor_tensor(scb[:], sco[:], eb_sb[:].unsqueeze(1).to_broadcast((P, NT, E)), ALU.add))
                    v = scb[:].rearrange("p t (g a c) -> p (t g) a c", a=2, c=2)
                    w = g1[:].rearrange("p t g w -> p (t g) w")
                    done(V.tensor_tensor(w[:, :, 0:2], v[:, :, :, 0], v[:, :, :, 1], ALU.max))
                    done(V.tensor_tensor(w[:, :, 2:4], v[:, :, :, 0], v[:, :, :, 1], ALU.min))
                    f = gs[:].rearrange("p t g -> p (t g)")
                    f2 = gm[:].rearrange("p t g -> p (t g)")
                    done(V.tensor_tensor(f, w[:, :, 2], w[:, :, 3], ALU.max))
                    done(V.tensor_tensor(f2, w[:, :, 0], w[:, :, 1], ALU.min))
                    done(V.tensor_tensor(f, f, f2, ALU.max))
                    done(V.tensor_tensor(f2, w[:, :, 0], w[:, :, 1], ALU.max))
                    done(V.tensor_tensor(f, f, f2, ALU.add))
                    own = gs[:].unsqueeze(3).to_broadcast((P, NT, NG, NG))
                    other = gs[:].unsqueeze(2).to_broadcast((P, NT, NG, NG))
                    done(V.tensor_tensor(bt[:], other, own, ALU.is_gt))
                    done(V.tensor_tensor(bt2[:], other, own, ALU.is_equal))
                    done(V.tensor_tensor(bt2[:], bt2[:], lt[:].unsqueeze(1).to_broadcast((P, NT, NG, NG)), ALU.mult))
                    done(V.tensor_tensor(bt[:], bt[:], bt2[:], ALU.add))
                    done(V.tensor_reduce(gm[:], bt[:], AX_X, ALU.add))
                    done(V.tensor_scalar(gm[:], gm[:], float(TOPG), None, ALU.is_lt))
                    done(V.tensor_tensor(scb[:].rearrange("p t (g c) -> p (t g) c", c=EG),
                                         scb[:].rearrange("p t (g c) -> p (t g) c", c=EG),
                                         gm[:].rearrange("p t g -> p (t g)").unsqueeze(2)
                                         .to_broadcast((P, NT * NG, EG)), ALU.mult), alone=True)
                    for t in range(NT):
                        last = V.max(top[:, t, :], scb[:, t, :])
                    done(last)
                    fourth = top[:, :, TOPK - 1:TOPK].to_broadcast((P, NT, E))
                    done(V.tensor_tensor(sel[:], scb[:], fourth, ALU.is_gt))
                    done(V.tensor_tensor(eq[:, 0, :, E:2 * E], scb[:], fourth, ALU.is_equal))
                    done(V.tensor_reduce(need[:], sel[:], AX_X, ALU.add))
                    done(V.tensor_scalar(need[:], need[:], -1.0, float(TOPK), ALU.mult, ALU.add))
                    done(V.tensor_copy(cmb[:], eq[:, 0, :, E:2 * E]))
                    for i, s in enumerate((1, 2, 4, 8)):
                        done(V.tensor_tensor(eq[:, (i + 1) % 2, :, E:2 * E], eq[:, i % 2, :, E:2 * E],
                                             eq[:, i % 2, :, E - s:2 * E - s], ALU.add))
                    done(V.tensor_tensor(eq[:, 0, :, E:2 * E], eq[:, 0, :, E:2 * E],
                                         need[:].unsqueeze(2).to_broadcast((P, NT, E)), ALU.is_le))
                    done(V.tensor_tensor(cmb[:], cmb[:], eq[:, 0, :, E:2 * E], ALU.mult))
                    done(V.tensor_tensor(sel[:], sel[:], cmb[:], ALU.add))
                    done(V.tensor_tensor(cmb[:], sel[:], sco[:], ALU.mult))
                    done(V.tensor_reduce(need[:], cmb[:], AX_X, ALU.add))
                    done(V.tensor_scalar(need[:], need[:], 1e-20, None, ALU.add))
                    done(V.reciprocal(need[:], need[:]))
                    done(V.tensor_scalar(need[:], need[:], ROUTE_SCALE, None, ALU.mult))
                    done(V.tensor_tensor(cmb[:], cmb[:], need[:].unsqueeze(2).to_broadcast((P, NT, E)), ALU.mult))
                    done(V.tensor_copy(cs[:, :, 0, :], cmb[:]))
                    V.tensor_tensor(cs[:, :, 1, :], cmb[:], cs[:, :, 0, :], ALU.subtract).then_inc(cs_rdy, 1)

                run(dve, slot, segment)


def kernel(**inputs):
    import numpy as _np
    import concourse.bacc as _bacc
    from concourse import mybir as _mybir
    from concourse.bass_utils import run_bass_kernel_spmd as _run

    a = {k.removeprefix("L0_"): _np.asarray(v) for k, v in inputs.items()}
    cat = _np.concatenate
    arrays = {
        "x": a["attn_tokens"],
        "wqkv": cat([a["attn_Wq"].reshape(P, 1, GROUPS, GW), a["attn_Wkv"].reshape(P, 2, GROUPS, GW)],
                    axis=1).transpose(0, 2, 1, 3).reshape(P, GROUPS, 3 * GW),
        "wo": a["attn_Wo"].reshape(PAIRS, P, P).transpose(1, 0, 2),
        "wg": cat([a["ffn_gate_w"].reshape(-1, P), a["ffn_sh_gate_w"]]).reshape(NJ, P, P).transpose(2, 0, 1),
        "wu": cat([a["ffn_up_w"].reshape(-1, P), a["ffn_sh_up_w"]]).reshape(NJ, P, P).transpose(2, 0, 1),
        "wd": cat([a["ffn_down_w"].transpose(0, 2, 1).reshape(-1, P), a["ffn_sh_down_w"].T])
        .reshape(NJ, P, P).transpose(1, 0, 2),
        "wr": a["ffn_router_weight"].T,
        "gq": a["attn_q_gamma"].reshape(1, HD),
        "gk": a["attn_k_gamma"].reshape(1, HD),
        "nw": a["attn_norm_w"].reshape(P, 1),
        "ebias": a["ffn_e_bias"].reshape(1, E),
        "cT": a["c"].T,
        "wmod": a["wmod"].reshape(P, 6, P),
    }
    nc = _bacc.Bacc("TRN2", target_bir_lowering=False, num_devices=1)
    given, args = {}, []
    for name, v in arrays.items():
        v = _np.ascontiguousarray(v)
        given[f"in_{name}"] = v
        args.append(nc.dram_tensor(f"in_{name}", v.shape, _mybir.dt.from_np(v.dtype), kind="ExternalInput").ap())
    args.append(nc.dram_tensor("out_0", (NB, SEQ, P), F32, kind="ExternalOutput").ap())
    block_kernel(nc, *args)
    r = _run(nc, [given], core_ids=[0])
    return r.results[0]["out_0"]
```

```python
from contextlib import ExitStack

import concourse.bass as bass
from concourse import mybir

F32 = mybir.dt.float32
F16 = mybir.dt.float16
F32R = mybir.dt.float32r
I32 = mybir.dt.int32
ALU = mybir.AluOpType
ACT = mybir.ActivationFunctionType
AX_X = mybir.AxisListType.X

P = 128
NB = 8
SEQ = 512
NT = SEQ // P
HEADS = 16
DH = 64
HD = HEADS * DH
GH = 4
GROUPS = HEADS // GH
GW = GH * DH
PAIRS = HEADS // 2
E = 16
NG = 4
EG = E // NG
TOPK = 4
TOPG = 2
I_MOE = 64
NJ = E * I_MOE // P + 1
SOFTCLAMP = 50.0
QSCALE = DH ** 0.5
LN_EPS = 1e-5
RMS_EPS = 1.1920928955078125e-07
NORM_MIN = 1e-12
SQUARES_ACT = HEADS + 11
RING = 2 * GH
UPPER = -4096
ROUTE_SCALE = 2.5
GATE_MIN = 0.25
FFN0 = 6
VEC_STEPS = 147
MAGIC = 1597463007.0


def block_kernel(nc, x, wqkv, wo, wg, wu, wd, wr, gq, gk, nw, ebias, cT, wmod, out):
    ctx = ExitStack()
    with ctx:
        def sb(name, shape, dt=F32):
            return ctx.enter_context(nc.sbuf_tensor(name, shape, dt))

        def ps(name, shape, dt=F32):
            return ctx.enter_context(nc.psum_tensor(name, shape, dt))

        def sem(name):
            return ctx.enter_context(nc.semaphore(name))

        wqkv_sb = [sb(f"wqkv_sb{i}", [P, GROUPS, 3 * GW], F32R) for i in range(2)]
        wo_sb = sb("wo_sb", [P, PAIRS, P])
        wg_sb = [sb(f"wg_sb{i}", [P, NJ, P], F32R) for i in range(2)]
        wu_sb = [sb(f"wu_sb{i}", [P, NJ, P], F32R) for i in range(2)]
        wd_sb = sb("wd_sb", [P, NJ, P])
        wr_sb = sb("wr_sb", [P, E])
        gam = sb("gam", [P, HD])
        nw_sb = sb("nw_sb", [P, 1])
        eb_sb = sb("eb_sb", [P, E])
        c_sb = sb("c_sb", [P, NB])
        cth = sb("cth", [P, NB])
        modT = sb("modT", [P, 6, NB])
        mtmp = sb("mtmp", [P, 2, NB])
        ident = sb("ident", [P, P])
        ident16 = sb("ident16", [P, P], F16)
        ones = sb("ones", [P, 1])
        expand = sb("expand", [P, NJ - 1, P], F16)
        lt = sb("lt", [P, NG, NG])

        NW = NT * 2 * GH
        x_in = sb("x_in", [P, NT, P])
        modA = sb("modA", [P, 6])
        modC = sb("modC", [P, 6])
        st = sb("st", [P, NT, 6])
        mv = sb("mv", [P, NT, 2])
        xh = sb("xh", [P, NT, P])
        hQ = [sb(f"hQ{i}", [P, SEQ], F32R) for i in range(2)]
        hV = [sb(f"hV{i}", [P, SEQ], F32R) for i in range(2)]
        sqT = xh[:].rearrange("p t d -> p (t d)")
        aux = sb("aux", [P, SEQ])
        hn = sb("hn", [P, NW])
        rV = sb("rV", [P, NT])
        clamp = sb("clamp", [P, NT])
        nx = sb("nx", [P, NW + 2 * NT])
        ny = sb("ny", [P, NW + 2 * NT])
        nt_ = sb("nt_", [P, NW + 2 * NT])
        ss = sb("ss", [P, 2, NT, 2 * GH])
        qk = sb("qk", [P, 2, NT, 2, GW])
        sq = sb("sq", [P, 2 * GW])
        qks = sb("qks", [P, 2, 2 * GH, 2, DH], F16)
        QK = sb("QK", [P, 2, RING, SEQ], F16)
        KS = sb("KS", [P, RING, SEQ], F16)
        Vh = sb("Vh", [P, NT, HEADS, DH + 1], F16)
        Vl = sb("Vl", [P, NT, HEADS, DH], F16)
        pr = sb("pr", [P, 2, NT, SEQ])
        ph = sb("ph", [P, 2, NT, SEQ], F16)
        pl = sb("pl", [P, 2, NT, SEQ], F16)
        rd = sb("rd", [P, NT])
        O_sb = sb("O_sb", [P, NT, 2, 2, DH])
        OT = sb("OT", [P, PAIRS, SEQ])
        aT = sb("aT", [P, SEQ])
        x1 = sb("x1", [P, NT, P])
        h2T = aux
        h2 = [sb(f"h2{i}", [P, SEQ], F32R) for i in range(2)]
        ex = sb("ex", [P, NT, E])
        sco = sb("sco", [P, NT, E])
        scb = sb("scb", [P, NT, E])
        g1 = sb("g1", [P, NT * NG, 6])
        gs = sb("gs", [P, NT, NG])
        bt = sb("bt", [P, NT * NG, 2, NG])
        gm = sb("gm", [P, NT, NG])
        top = sb("top", [P, NT, 8])
        sel = sb("sel", [P, NT, E])
        eq = sb("eq", [P, 3, NT, 2 * E])
        need = sb("need", [P, NT])
        cmb = sb("cmb", [P, NT, E])
        cs = sb("cs", [P, NT, 2, E], F16)
        cT_sb = sb("cT_sb", [P, SEQ], F16)
        th = sqT[:, 0:SEQ // 2]
        ga_ = sqT[:, SEQ // 2:SEQ]
        hb = sb("hb", [P, SEQ])
        hj = sb("hj", [P, 2, SEQ])
        upQ, up2 = hj[:, 0], hj[:, 1]
        o_sb = hb[:].rearrange("p (t d) -> p t d", d=P)
        gq_sb = pr[:, 0].rearrange("p a q -> p (a q)")[:, 0:HD]
        ph32 = ph[:].rearrange("p k a q -> p (k a q)").bitcast(F32)
        pl32 = pl[:].rearrange("p k a q -> p (k a q)").bitcast(F32)
        spread0 = ph32[:, 0:HD]
        wmod_sb = ph32[:, HD:HD + 6 * P].rearrange("p (j d) -> p j d", j=6)
        wqkv_in = pr[:].rearrange("p k a q -> p (k a q)")[:, HD:HD + 3 * HD]
        wg_in, wu_in = (OT[:].rearrange("p j q -> p (j q)")[:, i * NJ * P:(i + 1) * NJ * P] for i in range(2))

        S = [ps(f"S{i}", [P, 2, SEQ]) for i in range(2)]
        O = ps("O", [P, SEQ])
        ACC = ps("ACC", [P, SEQ])
        M6 = ps("M6", [P, SEQ])
        M7 = ps("M7", [P, SEQ])
        T16 = M6[:, :].bitcast(F16).rearrange("p (h t) -> p h t", t=P)
        C16 = ACC[:, :].bitcast(F16)

        def proj_banks(b):
            return (O, ACC) if isinstance(b, int) and b < 0 else (M6, M6)

        ld_c, ld_mod, ld_qkv, ld_nw, ld_gk, ld_gq = map(sem, ("ld_c", "ld_mod", "ld_qkv", "ld_nw", "ld_gk", "ld_gq"))
        ld_wo, ld_eb, ld_wr, ld_wg, ld_wu, ld_wd = map(sem, ("ld_wo", "ld_eb", "ld_wr", "ld_wg", "ld_wu", "ld_wd"))
        x_ld = sem("x_ld")
        built = sem("built")
        vec0 = sem("vec0")
        silu_c = sem("silu_c")
        modp = sem("modp")
        with nc.Block() as block:
            @block.sync
            def _(sp):
                for dst, src, done in ((c_sb[:], cT, ld_c), (nw_sb[:], nw, ld_nw), (wmod_sb, wmod, ld_mod),
                                       (x_in[:], x[0].rearrange("(t p) d -> p t d", p=P), x_ld),
                                       (wqkv_in, wqkv.rearrange("p g n -> p (g n)"), ld_qkv),
                                       (gam[:], gk.to_broadcast((P, HD)), ld_gk),
                                       (gq_sb, gq.to_broadcast((P, HD)), ld_gq), (wo_sb[:], wo, ld_wo),
                                       (eb_sb[:], ebias.to_broadcast((P, E)), ld_eb), (wr_sb[:], wr, ld_wr),
                                       (wg_in, wg.rearrange("p j d -> p (j d)"), ld_wg),
                                       (wu_in, wu.rearrange("p j d -> p (j d)"), ld_wu), (wd_sb[:], wd, ld_wd)):
                    sp.dma_start(dst, src).then_inc(done, 16)

            @block.gpsimd
            def _(pool):
                pool.memset(ident[:], 0.0).then_inc(built, 1)
                pool.memset(expand[:], 1.0).then_inc(built, 1)
                pool.memset(lt[:], 1.0).then_inc(built, 1)
                pool.memset(ones[:], 1.0).then_inc(built, 1)
                pool.memset(eq[:, :, :, 0:E], 0.0).then_inc(built, 1)
                pool.memset(cT_sb[:], 0.0).then_inc(built, 1)
                pool.memset(Vh[:, :, :, DH:DH + 1], 1.0).then_inc(built, 1)
                pool.wait_ge(built, 7)
                pool.affine_select(out=ident[:], in_=ident[:], compare_op=ALU.not_equal, fill=1.0,
                                   base=0, pattern=[[-1, P]], channel_multiplier=1).then_inc(built, 1)
                pool.memset(spread0, 0.0).then_inc(built, 1)
                pool.wait_ge(built, 9)
                for r in range(2):
                    v = spread0.rearrange("p (e i) -> p e i", i=I_MOE)
                    pool.affine_select(out=v, in_=v, compare_op=ALU.not_equal, fill=1.0,
                                       base=-E * r, pattern=[[-1, E], [0, I_MOE]],
                                       channel_multiplier=1).then_inc(built, 1)
                    pool.wait_ge(built, 10 + r)
                pool.affine_select(out=lt[:], in_=lt[:], compare_op=ALU.is_ge, fill=0.0,
                                   base=-1, pattern=[[1, NG], [-1, NG]],
                                   channel_multiplier=0).then_inc(built, 1)

            @block.vector
            def _(dve):
                n = [0]

                def done(ins):
                    n[0] += 1
                    ins.then_inc(vec0, 1)
                    dve.wait_ge(vec0, n[0])

                dve.wait_ge(built, 12)
                done(nc.vector.tensor_copy(ident16[:], ident[:]))
                done(nc.vector.tensor_copy(expand[:].rearrange("p j f -> p (j f)"), spread0))
                dve.wait_ge(silu_c, 1)
                done(nc.vector.scalar_tensor_tensor(cth[:], cth[:], 1.0, c_sb[:], ALU.add, ALU.mult))
                nc.vector.tensor_scalar(cth[:], cth[:], 0.5, None, ALU.mult).then_inc(silu_c, 1)
                dve.wait_ge(modp, 1)
                m = M7[:, 0:6 * NB].rearrange("p (j b) -> p j b", j=6)
                done(nc.vector.tensor_copy(modT[:], m))
                for j in (1, 4):
                    done(nc.vector.tensor_scalar(modT[:, j, :], modT[:, j, :], 1.0, None, ALU.add))
                for j in (2, 5):
                    g = modT[:, j, :]
                    done(nc.vector.tensor_scalar(mtmp[:, 0, :], g, 0.0, 2.0, ALU.is_ge, ALU.mult))
                    done(nc.vector.tensor_scalar(mtmp[:, 0, :], mtmp[:, 0, :], -1.0, None, ALU.add))
                    done(nc.vector.tensor_tensor(mtmp[:, 1, :], g, mtmp[:, 0, :], ALU.mult))
                    done(nc.vector.tensor_scalar(mtmp[:, 1, :], mtmp[:, 1, :], GATE_MIN, None, ALU.max))
                    done(nc.vector.tensor_tensor(g, mtmp[:, 1, :], mtmp[:, 0, :], ALU.mult))

            @block.scalar
            def _(act):
                act.wait_ge(ld_c, 16)
                nc.scalar.activation(cth[:], c_sb[:], ACT.Tanh, scale=0.5).then_inc(silu_c, 1)

            @block.tensor
            def _(pe):
                pe.wait_ge(silu_c, 2)
                pe.wait_ge(ld_mod, 16)
                for j in range(6):
                    last = nc.tensor.matmul(M7[:, j * NB:(j + 1) * NB], wmod_sb[:, j, :], cth[:],
                                            start=True, stop=True)
                last.then_inc(modp, 1)

        xr_ld = sem("xr_ld")
        k_swap = [sem(f"k_swap{g}") for g in range(GROUPS)]
        stored = sem("stored")
        w_rdy = sem("w_rdy")
        gam_rdy = sem("gam_rdy")
        vec = sem("vec")
        xh_rdy = sem("xh_rdy")
        sq_rdy = sem("sq_rdy")
        ms_rdy = sem("ms_rdy")
        rV_rdy = sem("rV_rdy")
        v_evac = sem("v_evac")
        ss_rdy = sem("ss_rdy")
        hn_rdy = sem("hn_rdy")
        plo_rdy = sem("plo_rdy")
        o_rdy = sem("o_rdy")
        aT_rdy = sem("aT_rdy")
        x1_sum = sem("x1_sum")
        x1_rdy = sem("x1_rdy")
        hQ_up, h2_up = sem("hQ_up"), sem("h2_up")
        cs_rdy = sem("cs_rdy")
        cT_rdy = sem("cT_rdy")
        gu_rd = sem("gu_rd")
        hj_rdy = sem("hj_rdy")
        yT_rdy = sem("yT_rdy")
        out_rdy = sem("out_rdy")
        xT_ps = sem("xT_ps")
        ms_ps = sem("ms_ps")
        qk_ps, v_ps = sem("qk_ps"), sem("v_ps")
        t_ps = sem("t_ps")
        s_ps = sem("s_ps")
        o_ps = sem("o_ps")
        ot_ps = sem("ot_ps")
        wo_ps = sem("wo_ps")
        at_ps = sem("at_ps")
        x2_ps = sem("x2_ps")
        lg_ps = sem("lg_ps")
        gu_ps = sem("gu_ps")
        ct_ps = sem("ct_ps")
        cb_ps = sem("cb_ps")
        dn_ps = sem("dn_ps")
        y_ps = sem("y_ps")
        qk_ev = sem("qk_ev")
        hV_rdy = sem("hV_rdy")
        v_ev = sem("v_ev")
        t_ev = sem("t_ev")
        tanh_d = sem("tanh_d")
        exp_d = sem("exp_d")
        ot_rdy = sem("ot_rdy")
        hQ_hi, h2_hi = sem("hQ_hi"), sem("h2_hi")
        h2_rdy = sem("h2_rdy")
        lg_ex = sem("lg_ex")
        th_d = sem("th_d")
        hQ_rdy = sem("hQ_rdy")
        h2_split = sem("h2_split")
        sqa_d = sem("sqa_d")
        sq_d = sem("sq_d")
        kg_d = sem("kg_d")
        qn_d = sem("qn_d")
        qhi_d = sem("qhi_d")
        qlo_rdy = sem("qlo_rdy")
        phi_d = sem("phi_d")

        l_gu, l_cb = sem("l_gu"), sem("l_cb")
        l_th = sem("l_th")
        l_h, l_hj = sem("l_h"), sem("l_hj")

        LAST = NB * HEADS

        held = sem("held")

        def live(b, h, ahead=0):
            return not isinstance(b, int) or 0 <= HEADS * b + h + ahead < LAST

        def act_squares(b):
            return isinstance(b, int) and b < 1

        def batch(b):
            return not isinstance(b, int) or 0 <= b < NB

        def first(b, n=1):
            return isinstance(b, int) and b < n

        def hold(eng, s, value):
            eng.wait_ge(s, value)
            if not isinstance(value, int):
                eng.sem_inc(held, 1)

        def run(eng, slot, last_features=None, segment=None):
            for b in (-1, 0, 1):
                for h in range(HEADS):
                    slot(b, h)
            if segment:
                segment(2)
            with eng.Fori(2, NB - 2) as b:
                for h in range(HEADS):
                    slot(b, h)
            if segment:
                segment(NB - 2)
            for b in (NB - 2, NB - 1):
                for h in range(HEADS):
                    slot(b, h)
            for h in range(FFN0):
                slot(NB, h)
            if last_features:
                last_features()
            for h in range(3):
                slot(NB + 1, h)

        with nc.Block() as block:
            @block.sync
            def _(sp):
                def slot(b, h):
                    if h == 1 and batch(b + 2):
                        sp.wait_ge(xh_rdy, (b + 2) * NT)
                        sp.dma_start(x_in[:], x[b + 2].rearrange("(t p) d -> p t d", p=P)).then_inc(x_ld, 16)
                    if h == 2 and batch(b - 2):
                        sp.wait_ge(out_rdy, b - 1)
                        sp.dma_start(out[b - 2].rearrange("(t p) d -> p t d", p=P), o_sb).then_inc(stored, 16)
                    if h == 2 and batch(b - 1):
                        if not first(b - 1):
                            sp.wait_ge(out_rdy, b - 1)
                        sp.dma_start(x1[:], x[b - 1].rearrange("(t p) d -> p t d", p=P)).then_inc(xr_ld, 16)
                    if h % GH == 2 and live(b, h, 2):
                        g = (h + 2) % HEADS // GH
                        hs = slice(GH * (g % 2), GH * (g % 2) + GH)
                        sp.wait_ge(t_ev, HEADS * b + h + 6)
                        sp.dma_start(KS[DH:P, hs, :], QK[0:DH, 1, hs, :]).then_inc(k_swap[g], 16)
                        sp.dma_start(KS[0:DH, hs, :], QK[DH:P, 1, hs, :]).then_inc(k_swap[g], 16)
                sp.sem_inc(stored, 16)
                run(sp, slot)
                sp.wait_ge(stored, 16 * (NB + 1))

            @block.gpsimd
            def _(pool):
                def slot(b, h):
                    i, s = h % GH, HEADS * b + h
                    if live(b, h, 11):
                        par, g, t = ((h + 11) // GH) % 2, (h + 11) % HEADS // GH, (h + 11) % NT
                        a = s + 11
                        hold(pool, qk_ev, a + 1)
                        if first(b, 0) and a == 0:
                            pool.wait_ge(gam_rdy, 1)
                        if act_squares(b):
                            pool.wait_ge(sqa_d, a + 1)
                        else:
                            hold(pool, ss_rdy, a)
                            nc.gpsimd.tensor_tensor(sq[:], qk[:, par, t].rearrange("p r n -> p (r n)"),
                                                    qk[:, par, t].rearrange("p r n -> p (r n)"),
                                                    ALU.mult).then_inc(sq_d, 1)
                            pool.wait_ge(sq_d, a + 1 - SQUARES_ACT)
                        nc.gpsimd.tensor_tensor(qk[:, par, t, 1], qk[:, par, t, 1], gam[:, GW * g:GW * g + GW],
                                                ALU.mult).then_inc(kg_d, 1)
                    if live(b, h):
                        hold(pool, exp_d, 2 * s + 2)
                        if not isinstance(b, int) or s >= 2:
                            hold(pool, o_ps, s - 1)
                        nc.gpsimd.tensor_scalar(ph[:, h % 2].rearrange("p a q -> p (a q)"),
                                                pr[:, h % 2].rearrange("p a q -> p (a q)"),
                                                1.0, 0.0, ALU.mult, ALU.add).then_inc(phi_d, 1)
                    if h == 3 and batch(b + 1):
                        if live(b, h, 12):
                            hold(pool, qk_ps, HEADS * b + h + 13)
                        pool.wait_ge(hQ_up, b + 2)
                        nc.gpsimd.tensor_tensor(hQ[1][:], aux[:], upQ, ALU.subtract).then_inc(hQ_rdy, 1)
                    if h == 5 and batch(b - 1):
                        pool.wait_ge(h2_up, b)
                        nc.gpsimd.tensor_tensor(h2[1][:], h2T[:], up2, ALU.subtract).then_inc(h2_split, 1)
                    if live(b, h, 7):
                        par, t, a = ((h + 7) // GH) % 2, (h + 7) % NT, s + 7
                        pool.wait_ge(hn_rdy, (GROUPS * b + (h + 7) // GH) + 1)
                        pool.wait_ge(kg_d, a + 1)
                        v = qk[:, par, t].rearrange("p r (h d) -> p (r h) d", d=DH)
                        nc.gpsimd.tensor_tensor(v, v, hn[:, t * 2 * GH:(t + 1) * 2 * GH].unsqueeze(2)
                                                .to_broadcast((P, 2 * GH, DH)), ALU.mult).then_inc(qn_d, 1)
                        hold(pool, qn_d, a + 1)
                        if live(b, h, 5):
                            hold(pool, t_ps, s + 5 + 1)
                        nc.gpsimd.tensor_scalar(qks[:, (h + 7) % 2, :, 0, :],
                                                qk[:, par, t].rearrange("p r (h d) -> p (r h) d", d=DH),
                                                1.0, 0.0, ALU.mult, ALU.add).then_inc(qhi_d, 1)
                        pool.wait_ge(qhi_d, a + 1)
                        nc.gpsimd.tensor_tensor(qks[:, (h + 7) % 2, :, 1, :],
                                                qk[:, par, t].rearrange("p r (h d) -> p (r h) d", d=DH),
                                                qks[:, (h + 7) % 2, :, 0, :], ALU.subtract).then_inc(qlo_rdy, 1)
                run(pool, slot)

            @block.scalar
            def _(act):
                def tanh(b, h, u):
                    if live(b, h, 1):
                        s, k = HEADS * b + h + 1, (h + 1) % 2
                        act.wait_ge(s_ps, 2 * s + u + 1)
                        if u == 0 and (not isinstance(b, int) or s >= 2):
                            act.wait_ge(plo_rdy, s - 1)
                        nc.scalar.activation(pr[:, k, 2 * u:2 * u + 2, :], S[u][:], ACT.Tanh,
                                             scale=QSCALE * QSCALE / SOFTCLAMP).then_inc(tanh_d, 1)

                def exponential(b, h, u):
                    if live(b, h):
                        s = HEADS * b + h
                        act.wait_ge(tanh_d, 2 * s + u + 1)
                        half = pr[:, h % 2, 2 * u:2 * u + 2, :]
                        nc.scalar.activation(half, half, ACT.Exp, scale=SOFTCLAMP * DH ** -0.5).then_inc(exp_d, 1)

                def slot(b, h):
                    i, s, c = h % GH, HEADS * b + h, b - 1
                    tile = h - FFN0
                    gate(b, tile, 0)
                    if live(b, h, 5):
                        g, t = (h + 5) % HEADS // GH, (h + 5) % NT
                        act.wait_ge(t_ps, s + 5 + 1)
                        nc.scalar.activation(QK[:, :, GH * (g % 2):GH * (g % 2) + GH, t * P:(t + 1) * P],
                                             T16.rearrange("p (r h) t -> p r h t", r=2), ACT.Copy).then_inc(t_ev, 1)
                    exponential(b, h, 1)
                    if live(b, h, 12):
                        par, a = ((h + 12) // GH) % 2, s + 12
                        act.wait_ge(qk_ps, a + 1)
                        if not isinstance(b, int) or a >= 8:
                            act.wait_ge(qlo_rdy, a - 8 + 1)
                        nc.scalar.activation(qk[:, par, i].rearrange("p r n -> p (r n)"), proj_banks(b)[0][:],
                                             ACT.Copy).then_inc(qk_ev, 1)
                        if isinstance(b, int) and a < SQUARES_ACT:
                            if a:
                                act.wait_ge(ss_rdy, a)
                            nc.scalar.activation(sq[:], proj_banks(b)[0][:], ACT.Square).then_inc(sqa_d, 1)
                    if h == 3 and batch(b + 1):
                        act.wait_ge(hQ_up, b + 2)
                        nc.scalar.activation(hQ[0][:], upQ, ACT.Copy).then_inc(hQ_hi, 1)
                    if h == 5 and batch(c):
                        act.wait_ge(h2_up, b)
                        nc.scalar.activation(h2[0][:], up2, ACT.Copy).then_inc(h2_hi, 1)
                    if tile:
                        gate(b, tile, 1)
                    tanh(b, h, 0)
                    if live(b, h, 8):
                        g, a = (h + 8) % HEADS // GH, s + 8
                        act.wait_ge(v_ps, a + 1)
                        if h == 8:
                            act.wait_ge(rV_rdy, b + 2)
                        nc.scalar.activation(Vh[:, i, GH * g:GH * g + GH, 0:DH],
                                             proj_banks(b)[1][:, 0:GW].rearrange("p (h d) -> p h d", d=DH), ACT.Copy,
                                             scale=rV[:, i:i + 1]).then_inc(v_ev, 1)
                    if tile == 0:
                        gate(b, tile, 1)
                    tanh(b, h, 1)
                    if h == 4 and batch(c):
                        act.wait_ge(x2_ps, b)
                        nc.scalar.activation(h2T[:], M7[:], ACT.Identity, scale=modC[:, 4:5],
                                             bias=modC[:, 3:4]).then_inc(h2_rdy, 1)
                    if h == 7 and batch(b + 1):
                        if live(b, h, 8):
                            act.wait_ge(v_ps, HEADS * b + h + 9)
                        act.wait_ge(hQ_rdy, b + 2)
                        for part in range(2):
                            nc.scalar.activation(hV[part][:], hQ[part][:], ACT.Copy).then_inc(hV_rdy, 1)
                    j = (h - 3) // 2
                    if h % 2 and live(b, h, -3):
                        n = PAIRS * b + j
                        act.wait_ge(ot_ps, n + 1)
                        if j == 0 and not first(b, 1):
                            act.wait_ge(wo_ps, b)
                        nc.scalar.activation(OT[:, j % PAIRS, :], M7[:], ACT.Copy).then_inc(ot_rdy, 1)
                    if batch(c) and h == 4:
                        act.wait_ge(lg_ps, b)
                        nc.scalar.activation(ex[:].rearrange("p t e -> p (t e)"), ACC[:, 0:NT * E], ACT.Exp,
                                             scale=-1.0).then_inc(lg_ex, 1)
                    if h + 1 < HEADS:
                        exponential(b, h + 1, 0)
                    else:
                        exponential(b + 1, 0, 0)

                def gate(b, tile, a):
                    if batch(b - 1) and 0 <= tile < NJ:
                        n = 2 * NJ * (b - 1) + 2 * tile + a
                        act.wait_ge(gu_ps, n + 1)
                        if not isinstance(b, int) or n:
                            act.wait_ge(gu_rd, n)
                        nc.scalar.activation(th, M7[:, 0:SEQ // 2], ACT.Tanh, scale=0.5).then_inc(th_d, 1)

                def last_features():
                    for j in range(NJ):
                        act.wait_ge(l_gu, j + 1)
                        if j >= 2:
                            act.wait_ge(l_h, j - 1)
                        nc.scalar.activation(pr[:, 0, j % 2, :], S[j % 2][:, 0, :], ACT.Tanh,
                                             scale=0.5).then_inc(l_th, 1)
                run(act, slot, last_features)

            @block.tensor
            def _(pe):
                mm = nc.tensor.matmul

                def mm3(dst, left, right):
                    mm(dst, left[0], right[0], start=True, stop=False)
                    mm(dst, left[0], right[1], start=False, stop=False)
                    return mm(dst, left[1], right[0], start=False, stop=True)

                def part(split, *at):
                    return [w[(slice(None),) + at] for w in split]

                def transpose4(dst, src):
                    for t in range(NT):
                        last = nc.tensor.transpose(dst[:, t * P:(t + 1) * P], src(t), ident[:])
                    return last

                def scores(b, h, u):
                    s, k = HEADS * b + h + 1, (h + 1) % HEADS
                    if k % GH == 0 and u == 0:
                        kb = b if h + 1 < HEADS else b + 1
                        pe.wait_ge(k_swap[k // GH], 32 * kb + 32)
                    if not isinstance(b, int) or s >= 1:
                        pe.wait_ge(tanh_d, 2 * (s - 1) + u + 1)
                    r = k % RING
                    for a in range(2):
                        ks = slice((2 * u + a) * P, (2 * u + a + 1) * P)
                        mm(S[u][:, a, :], QK[:, 1, r, ks], QK[:, 0, r, :], start=True, stop=False)
                        last = mm(S[u][:, a, :], KS[:, r, ks], QK[:, 0, r, :], start=False, stop=True)
                    last.then_inc(s_ps, 1)

                def values(b, h):
                    s, k = HEADS * b + h - 1, (h - 1) % HEADS
                    pe.wait_ge(plo_rdy, s + 1)
                    pe.wait_ge(v_evac, s - k % GH + GH)
                    if not isinstance(b, int) or s >= 1:
                        pe.wait_ge(o_rdy, s)
                    for c in range(NT):
                        o = O[:, c * (DH + 1):(c + 1) * (DH + 1)]
                        qs = slice(c * P, (c + 1) * P)
                        for t in range(NT):
                            mm(o, ph[:, k % 2, t, qs], Vh[:, t, k, :], start=(t == 0), stop=False)
                            mm(o[:, 0:DH], ph[:, k % 2, t, qs], Vl[:, t, k, :], start=False, stop=False)
                            last = mm(o, pl[:, k % 2, t, qs], Vh[:, t, k, :], start=False, stop=(t == NT - 1))
                    last.then_inc(o_ps, 1)

                def slot(b, h):
                    i, s, c = h % GH, HEADS * b + h, b - 1
                    tile = h - FFN0
                    ffn = batch(c) and 0 <= tile < NJ
                    if ffn and h % 2:
                        gate_up(b, tile, 0)
                    if live(b, h, 5):
                        pe.wait_ge(qlo_rdy, s + 5 + 1)
                        if live(b, h, 7) and not first(b, 0):
                            pe.wait_ge(v_evac, s + 8)
                        elif live(b, h, 4):
                            pe.wait_ge(t_ev, s + 5)
                        for n in range(2 * GH):
                            last = nc.tensor.transpose(T16[:, n, :],
                                                       qks[:, (h + 5) % 2, n].rearrange("p a d -> p (a d)"),
                                                       ident16[:])
                        last.then_inc(t_ps, 1)
                    if ffn and h % 2 == 0:
                        gate_up(b, tile, 0)
                    if h == 2 and batch(b + 1):
                        pe.wait_ge(xh_rdy, NT * (b + 2))
                        if live(b, h, -3):
                            pe.wait_ge(ot_rdy, PAIRS * b)
                        transpose4(M7, lambda t: xh[:, t, :]).then_inc(xT_ps, 1)
                    if live(b, h, 1):
                        scores(b, h, 0)
                    if batch(c) and 2 <= tile <= NJ:
                        down(b, tile - 1)
                    if h == FFN0 + 1 and batch(c):
                        pe.wait_ge(cs_rdy, b)
                        for t in range(NT):
                            last = nc.tensor.transpose(C16[0:2 * E, t * P:(t + 1) * P],
                                                       cs[:, t].rearrange("p a e -> p (a e)"), ident16[:])
                        last.then_inc(ct_ps, 1)
                    if h == 2 and batch(c):
                        output_projection(b, 6, PAIRS)
                    if live(b, h, 12):
                        g = (h + 12) % HEADS // GH
                        if h == 4:
                            pe.wait_ge(hQ_hi, b + 2)
                            pe.wait_ge(hQ_rdy, b + 2)
                        if first(b, 0):
                            if live(b, h, 11):
                                pe.wait_ge(sqa_d, s + 12)
                        elif live(b, h, 5):
                            pe.wait_ge(t_ev, s + 5 + 1)
                        elif live(b, h, 7):
                            pe.wait_ge(v_evac, s + 8)
                        elif live(b, h, 11):
                            pe.wait_ge(qk_ev, s + 12)
                        if isinstance(b, int) and s + 12 in range(0, HEADS, GH):
                            pe.wait_ge(w_rdy, g + 1 if g < 3 else GROUPS + 2)
                        mm3(proj_banks(b)[0][:], part(hQ, slice(i * P, (i + 1) * P)),
                            part(wqkv_sb, g, slice(0, 2 * GW))).then_inc(qk_ps, 1)
                    if ffn and tile:
                        gate_up(b, tile, 1)
                    if live(b, h, 1):
                        scores(b, h, 1)
                    if live(b, h, 8):
                        g = (h + 8) % HEADS // GH
                        if h == 8:
                            pe.wait_ge(hV_rdy, 2 * (b + 2))
                        if first(b, 0):
                            if live(b, h, 7):
                                pe.wait_ge(v_evac, s + 8)
                        elif live(b, h, 12):
                            pe.wait_ge(qk_ev, s + 13)
                            if isinstance(b, int) and s + 12 < SQUARES_ACT:
                                pe.wait_ge(sqa_d, s + 13)
                        elif live(b, h, 5):
                            pe.wait_ge(t_ev, s + 6)
                        mm3(proj_banks(b)[1][:, 0:GW], part(hV, slice(i * P, (i + 1) * P)),
                            part(wqkv_sb, g, slice(2 * GW, 3 * GW))).then_inc(v_ps, 1)
                    if h == 4 and batch(c):
                        pe.wait_ge(x1_rdy, NT * b)
                        if live(b, h, -4):
                            pe.wait_ge(ot_rdy, PAIRS * b + 1)
                        transpose4(M7, lambda t: xh[:, t, :]).then_inc(x2_ps, 1)
                    if ffn and tile == 0:
                        gate_up(b, tile, 1)
                    if ffn and tile:
                        spread(b, tile)
                    if live(b, h, -1):
                        values(b, h)
                    if h == 2 and batch(b + 1):
                        pe.wait_ge(sq_rdy, b + 2)
                        for t in range(NT):
                            last = mm(M7[:, t:t + 1], sqT[:, t * P:(t + 1) * P], ones[:], start=True, stop=True)
                        last.then_inc(ms_ps, 1)
                    if h % 2 and live(b, h, -3):
                        n, pj = PAIRS * b + (h - 3) // 2, ((h - 3) // 2) % 2
                        pe.wait_ge(o_rdy, 2 * n + 2)
                        before_pair(b, h)
                        transpose4(M7, lambda t: O_sb[:, t, pj].rearrange("p e d -> p (e d)")).then_inc(ot_ps, 1)
                    late(b, h)

                def before_pair(b, h):
                    c = b - 1
                    if h == 1:
                        pe.wait_ge(ot_rdy, PAIRS * b - 1)
                        if batch(b - 2):
                            pe.wait_ge(out_rdy, b - 1)
                    elif h == 3:
                        if batch(b + 1):
                            pe.wait_ge(ms_rdy, b + 2)
                    elif h == 5 and batch(c):
                        pe.wait_ge(h2_rdy, b)
                    elif batch(c) and h == FFN0 + 1:
                        pe.wait_ge(hj_rdy, (NJ - 1) * c + 1)
                    elif batch(c) and h < HEADS - 1:
                        pe.wait_ge(hj_rdy, (NJ - 1) * c + h - FFN0)
                    elif h == HEADS - 1 and batch(c):
                        pe.wait_ge(hj_rdy, (NJ - 1) * c + NJ - 1)
                    elif h >= 5:
                        pe.wait_ge(ot_rdy, PAIRS * b + (h - 3) // 2)

                def output_projection(b, lo, hi):
                    pe.wait_ge(ot_rdy, PAIRS * (b - 1) + hi)
                    for j in range(lo, hi):
                        last = mm(ACC[:], wo_sb[:, j, :], OT[:, j, :], start=(j == 0), stop=(j == PAIRS - 1))
                    if hi == PAIRS:
                        last.then_inc(wo_ps, 1)

                def gate_up(b, tile, a):
                    c = b - 1
                    w = NJ - 1 if tile == 0 else tile - 1
                    h = FFN0 + tile
                    n = 2 * NJ * c + 2 * tile + a
                    if a == 1:
                        pe.wait_ge(gu_rd, n)
                    elif tile == 0:
                        if first(c):
                            pe.wait_ge(w_rdy, GROUPS + 2)
                            pe.wait_ge(ld_wd, 16)
                        pe.wait_ge(h2_hi, b)
                        pe.wait_ge(h2_split, b)
                        if live(b, h, -4):
                            pe.wait_ge(ot_rdy, PAIRS * b + 2)
                    else:
                        if tile == 1:
                            pe.wait_ge(gu_rd, n)
                        else:
                            pe.wait_ge(hj_rdy, (NJ - 1) * c + tile - 1)
                        if h % 2 == 0 and live(b, h, -4):
                            pe.wait_ge(ot_rdy, PAIRS * b + (h - 4) // 2 + 1)
                    q = slice(a * SEQ // 2, (a + 1) * SEQ // 2)
                    mm3(M7[:, 0:SEQ // 2], part(wg_sb, w), part(h2, q))
                    mm3(M7[:, SEQ // 2:SEQ], part(wu_sb, w), part(h2, q)).then_inc(gu_ps, 1)

                def spread(b, tile):
                    c = b - 1
                    pe.wait_ge(gu_rd, 2 * NJ * c + 2 * tile + 2)
                    if tile == 1:
                        pe.wait_ge(cT_rdy, b)
                    mm(M7[:], expand[:, tile - 1, :], cT_sb[:], start=True, stop=True).then_inc(cb_ps, 1)

                def late(b, h):
                    c = b - 1
                    if h == 0 and batch(b - 2):
                        pe.wait_ge(yT_rdy, b - 1)
                        if live(b, h, -3):
                            pe.wait_ge(ot_rdy, PAIRS * b - 1)
                        transpose4(M7, lambda t: aT[:, t * P:(t + 1) * P]).then_inc(y_ps, 1)
                    if not batch(c):
                        return
                    if h == 0:
                        if first(c):
                            pe.wait_ge(ld_wo, 16)
                        output_projection(b, 0, 3)
                    if h == 1:
                        output_projection(b, 3, 6)
                    if h == 2:
                        pe.wait_ge(aT_rdy, b)
                        transpose4(ACC, lambda t: aT[:, t * P:(t + 1) * P]).then_inc(at_ps, 1)
                    if h == 4:
                        if first(c):
                            pe.wait_ge(ld_wr, 16)
                        pe.wait_ge(h2_rdy, b)
                        for t in range(NT):
                            last = mm(ACC[:, t * E:(t + 1) * E], h2T[:, t * P:(t + 1) * P], wr_sb[:],
                                      start=True, stop=True)
                        last.then_inc(lg_ps, 1)
                    if h == FFN0 + 1:
                        down(b, 0)

                def down(b, tile):
                    c = b - 1
                    w = NJ - 1 if tile == 0 else tile - 1
                    if tile:
                        pe.wait_ge(hj_rdy, (NJ - 1) * c + tile)
                    else:
                        pe.wait_ge(gu_rd, 2 * NJ * c + 2)
                        pe.wait_ge(cT_rdy, b)
                    mm(ACC[:], wd_sb[:, w, :], hj[:, tile % 2, :], start=(tile == 0),
                       stop=(tile == NJ - 1)).then_inc(dn_ps, 1)

                def last_features():
                    def down(j):
                        w = NJ - 1 if j == 0 else j - 1
                        if j:
                            pe.wait_ge(l_hj, j)
                        else:
                            pe.wait_ge(l_h, 1)
                        mm(ACC[:], wd_sb[:, w, :], hj[:, j % 2, :], start=(j == 0),
                           stop=(j == NJ - 1)).then_inc(dn_ps, 1)

                    pe.wait_ge(h2_hi, NB)
                    pe.wait_ge(h2_split, NB)
                    pe.wait_ge(tanh_d, 2 * LAST)
                    for j in range(NJ):
                        w = NJ - 1 if j == 0 else j - 1
                        if j >= 2:
                            pe.wait_ge(l_h, j - 1)
                        mm3(S[j % 2][:, 0, :], part(wg_sb, w), part(h2))
                        mm3(S[j % 2][:, 1, :], part(wu_sb, w), part(h2)).then_inc(l_gu, 1)
                        if j == 1:
                            pe.wait_ge(cs_rdy, NB)
                            for t in range(NT):
                                last = nc.tensor.transpose(C16[0:2 * E, t * P:(t + 1) * P],
                                                           cs[:, t].rearrange("p a e -> p (a e)"), ident16[:])
                            last.then_inc(ct_ps, 1)
                        if j:
                            pe.wait_ge(cT_rdy, NB)
                            if j >= 3:
                                pe.wait_ge(l_hj, j - 2)
                            mm((M6, M7)[j % 2][:], expand[:, j - 1, :], cT_sb[:], start=True,
                               stop=True).then_inc(l_cb, 1)
                        if j >= 2:
                            down(j - 2)
                    down(NJ - 2)
                    down(NJ - 1)

                run(pe, slot, last_features)

            @block.vector
            def _(dve):
                V = nc.vector
                at = [0, 0, None]

                def done(ins):
                    at[1] += 1
                    return ins.then_inc(vec, 1)

                def settled(alone=False):
                    b = at[2]
                    value = at[0] + at[1] if b is None else (b - 2) * VEC_STEPS + (at[0] + at[1])
                    if alone:
                        hold(dve, vec, value)
                    else:
                        dve.wait_ge(vec, value)
                    return V

                def segment(b):
                    if b > 2:
                        assert at[1] == VEC_STEPS, at[1]
                        at[0], at[1], at[2] = at[0] + (NB - 4) * VEC_STEPS, 0, None
                    else:
                        at[0], at[1] = at[0] + at[1], 0

                def inverse_root(cols, steps):
                    X, Y, T = nx[:, cols], ny[:, cols], nt_[:, cols]
                    for k in steps:
                        v = settled()
                        if k == 0:
                            done(v.tensor_single_scalar(T.bitcast(I32), X.bitcast(I32), 1, ALU.arith_shift_right))
                        elif k == 1:
                            done(v.tensor_scalar(Y.bitcast(I32), T.bitcast(I32), -1.0, MAGIC, ALU.mult, ALU.add))
                        elif k % 3 == 2:
                            done(v.scalar_tensor_tensor(T, Y, -0.5, Y, ALU.mult, ALU.mult))
                        elif k % 3 == 0:
                            done(v.tensor_tensor(T, T, X, ALU.mult))
                        else:
                            done(v.scalar_tensor_tensor(Y, T, 1.5, Y, ALU.add, ALU.mult))

                LN1 = slice(NW, NW + NT)
                LN2 = slice(NW + NT, NW + 2 * NT)

                def moments(src, cols):
                    for t in range(NT):
                        done(V.bn_stats(st[:, t, :], src[:, t, :]))
                    settled(alone=True)
                    for t in range(NT):
                        done(V.bn_aggr(mv[:, t, :], st[:, t, :]))
                    done(settled().tensor_scalar(nx[:, cols], mv[:, :, 1], LN_EPS, None, ALU.add))

                def standardize(src, cols, t, ready):
                    V.tensor_scalar(xh[:, t, :], src[:, t, :], mv[:, t, 0:1], ny[:, cols][:, t:t + 1],
                                    ALU.subtract, ALU.mult).then_inc(ready, 1)

                def split_weights(dst, src, width):
                    up = pl32[:, 0:width]
                    done(V.tensor_single_scalar(up.bitcast(I32), src.bitcast(I32), UPPER, ALU.bitwise_and))
                    done(settled().tensor_copy(dst[0], up))
                    V.tensor_tensor(dst[1], src, up, ALU.subtract).then_inc(w_rdy, 1)

                def split_projection(g):
                    w = wqkv_in[:, 3 * GW * g:3 * GW * (g + 1)]
                    done(settled().tensor_scalar(w, w, nw_sb[:], None, ALU.mult))
                    settled()
                    split_weights([x[:, g, :] for x in wqkv_sb], w, 3 * GW)

                def slot(b, h):
                    at[2] = None if isinstance(b, int) else b
                    if first(b, 0):
                        if h == 4:
                            dve.wait_ge(ld_nw, 16)
                            dve.wait_ge(ld_qkv, 16)
                        if h in (4, 6, 9, 14):
                            split_projection((4, 6, 9, 14).index(h))
                        if h in (10, 11):
                            w, w_in, ld = ((wg_sb, wg_in, ld_wg), (wu_sb, wu_in, ld_wu))[h - 10]
                            dve.wait_ge(ld, 16)
                            dve.wait_ge(w_rdy, h - 7)
                            split_weights([x[:].rearrange("p j d -> p (j d)") for x in w], w_in, NJ * P)
                        if h == 5:
                            dve.wait_ge(ld_gk, 16)
                            dve.wait_ge(ld_gq, 16)
                            done(V.tensor_scalar(gq_sb, gq_sb, 1.0, None, ALU.add))
                            settled().scalar_tensor_tensor(gam[:], gam[:], 1.0, gq_sb, ALU.add,
                                                           ALU.mult).then_inc(gam_rdy, 1)
                    i, s, c = h % GH, HEADS * b + h, b - 1
                    tile = h - FFN0
                    ffn = batch(c) and 0 <= tile < NJ
                    between(b, h, 0)
                    if ffn:
                        hidden(b, tile, 0)
                    if live(b, h, 11):
                        par, t = ((h + 11) // GH) % 2, (h + 11) % NT
                        if act_squares(b):
                            dve.wait_ge(sqa_d, s + 11 + 1)
                        else:
                            dve.wait_ge(sq_d, s + 11 + 1 - SQUARES_ACT)
                        V.tensor_reduce(ss[:, par, t, :], sq[:].rearrange("p (h d) -> p h d", d=DH),
                                        AX_X, ALU.add).then_inc(ss_rdy, 1)
                    between(b, h, 1)
                    between(b, h, 2)
                    if ffn and tile:
                        hidden(b, tile, 1)
                    between(b, h, 3)
                    if live(b, h, 8):
                        g = (h + 8) % HEADS // GH
                        dve.wait_ge(v_ev, s + 8 + 1)
                        V.scalar_tensor_tensor(Vl[:, i, GH * g:GH * g + GH, :],
                                               proj_banks(b)[1][:, 0:GW].rearrange("p (h d) -> p h d", d=DH),
                                               rV[:, i:i + 1],
                                               Vh[:, i, GH * g:GH * g + GH, 0:DH],
                                               ALU.mult, ALU.subtract).then_inc(v_evac, 1)
                    if ffn and tile == 0:
                        hidden(b, tile, 1)
                    between(b, h, 4)
                    if ffn and tile:
                        n = NJ * c + tile
                        dve.wait_ge(cb_ps, (NJ - 1) * c + tile)
                        if not isinstance(b, int) or n >= 2:
                            dve.wait_ge(dn_ps, n - 1)
                        V.tensor_tensor(hj[:, tile % 2, :], hb[:], M7[:], ALU.mult).then_inc(hj_rdy, 1)
                    if live(b, h):
                        dve.wait_ge(phi_d, s + 1)
                        V.tensor_tensor(pl[:, h % 2], pr[:, h % 2], ph[:, h % 2], ALU.subtract).then_inc(plo_rdy, 1)
                    between(b, h, 5)
                    if live(b, h, -1):
                        k = (h - 1) % HEADS
                        dve.wait_ge(o_ps, s)
                        if not isinstance(b, int) or s >= 2:
                            dve.wait_ge(o_rdy, s - 1)
                        if k % 2 == 0 and (not isinstance(b, int) or s >= 5):
                            dve.wait_ge(ot_ps, PAIRS * b + (h - 3) // 2)
                        o = O[:, 0:NT * (DH + 1)].rearrange("p (c d) -> p c d", d=DH + 1)
                        done(V.reciprocal(rd[:], o[:, :, DH]))
                        between(b, h, 6)
                        settled().tensor_tensor(O_sb[:, :, (k // 2) % 2, k % 2, :], o[:, :, 0:DH],
                                                rd[:].unsqueeze(2).to_broadcast((P, NT, DH)),
                                                ALU.mult).then_inc(o_rdy, 1)
                    else:
                        between(b, h, 6)
                    between(b, h, 7)

                def hidden(b, tile, a):
                    c = b - 1
                    n = 2 * NJ * c + 2 * tile + a
                    q = slice(a * SEQ // 2, (a + 1) * SEQ // 2)
                    dve.wait_ge(th_d, n + 1)
                    if not isinstance(b, int) or n:
                        dve.wait_ge(gu_rd, n)
                    done(V.scalar_tensor_tensor(ga_, th, 1.0, M7[:, 0:SEQ // 2], ALU.add, ALU.mult))
                    if a == 0 and tile >= 2:
                        dve.wait_ge(hj_rdy, (NJ - 1) * c + tile - 1)
                    if a == 0 and tile == 1:
                        dve.wait_ge(stored, 16 * b)
                    dst = hb if tile else hj[:, 0]
                    settled().scalar_tensor_tensor(dst[:, q], ga_, 0.5, M7[:, SEQ // 2:SEQ], ALU.mult,
                                                   ALU.mult).then_inc(gu_rd, 1)

                def last_features():
                    for step in range(7, 14):
                        route(step)
                    def weigh(j):
                        dve.wait_ge(l_cb, j)
                        dve.wait_ge(l_h, j + 1)
                        if j >= 2:
                            dve.wait_ge(dn_ps, NJ * (NB - 1) + j - 1)
                        V.tensor_tensor(hj[:, j % 2, :], pr[:, 1, j % 2, :], (M6, M7)[j % 2][:],
                                        ALU.mult).then_inc(l_hj, 1)

                    for j in range(NJ):
                        g, product = pr[:, 0, 2 + j % 2, :], pr[:, 1, j % 2, :]
                        dve.wait_ge(l_th, j + 1)
                        if j >= 2:
                            dve.wait_ge(l_h, j - 1)
                        done(V.scalar_tensor_tensor(g, pr[:, 0, j % 2, :], 1.0, S[j % 2][:, 0, :], ALU.add, ALU.mult))
                        if j == 1:
                            dve.wait_ge(ct_ps, NB)
                            V.tensor_copy(cT_sb[0:2 * E, :], C16[0:2 * E, 0:SEQ]).then_inc(cT_rdy, 1)
                        if j >= 2:
                            weigh(j - 1)
                        if j >= 3:
                            dve.wait_ge(l_hj, j - 2)
                        settled().scalar_tensor_tensor(product if j else hj[:, 0], g, 0.5, S[j % 2][:, 1, :], ALU.mult,
                                                       ALU.mult).then_inc(l_h, 1)
                    weigh(NJ - 1)

                def between(b, h, p):
                    c = b - 1
                    norms = h % GH == 0 and live(b, h, 8)
                    tokens = h in (0, 4) and batch(b + 1)
                    if h == 4 and p == 0 and tokens:
                        dve.wait_ge(ms_rdy, b + 2)
                    if norms or tokens:
                        cols = slice(0 if norms else NW, NW + NT if tokens else NW)
                        if p == 1 and h == 0:
                            settled()
                        if p == 1 and norms:
                            par = ((h + 8) // GH) % 2
                            dve.wait_ge(ss_rdy, HEADS * b + h + 8 + GH)
                            done(settled().tensor_tensor(nx[:, 0:NW].rearrange("p (t n) -> p t n", n=2 * GH),
                                                         ss[:, par], clamp[:].unsqueeze(2).to_broadcast((P, NT, 2 * GH)), ALU.max))
                        if h in (0, 4):
                            inverse_root(cols, ((), (0, 1, 2), (3, 4, 5), (6,), (7,), (8,), (9,), (10,))[p])
                        else:
                            inverse_root(cols, ((), (0, 1, 2), (3, 4, 5), (6,), (7,), (), (), ())[p])
                    if h in (9, 13) and p == 1 and live(b, h, 7):
                        inverse_root(slice(0, NW), (8, 9, 10))
                    if norms and h in (0, 4) and p == 7 or h in (9, 13) and live(b, h, 7) and p == 2:
                        if live(b, h - h % GH, 7):
                            dve.wait_ge(qn_d, HEADS * b + h - h % GH + 8)
                        settled().tensor_copy(hn[:], ny[:, 0:NW]).then_inc(hn_rdy, 1)
                    if h == 0 and first(b, 0) and p == 0:
                        dve.wait_ge(x_ld, 16)
                        moments(x_in, LN1)
                    if h == HEADS - 1 and p == 3 and batch(b + 2):
                        dve.wait_ge(x_ld, 16 * (b + 3))
                        moments(x_in, LN1)
                    if batch(b + 1):
                        ahead(b, h, p)
                    if batch(b - 2):
                        if h == 0 and p == 2:
                            dve.wait_ge(dn_ps, NJ * (b - 1))
                            V.tensor_scalar(aT[:], ACC[:], modC[:, 5:6], None, ALU.mult).then_inc(yT_rdy, 1)
                        if h == 1 and p == 1:
                            dve.wait_ge(y_ps, b - 1)
                            dve.wait_ge(stored, 16 * (b - 1))
                            V.tensor_tensor(o_sb.rearrange("p t d -> p (t d)"), M7[:],
                                            x1[:].rearrange("p t d -> p (t d)"), ALU.add).then_inc(out_rdy, 1)
                    if batch(c):
                        behind(b, h, p)

                def ahead(b, h, p):
                    if h == 1 and p in (0, 1, 2, 3):
                        if p == 0:
                            done(settled().tensor_copy(modA[:],
                                                       modT[:, :, bass.ds(b + 1, 1)].rearrange("p j b -> p (j b)")))
                        standardize(x_in, LN1, p, xh_rdy)
                    if h == 2 and p == 1:
                        dve.wait_ge(xT_ps, b + 2)
                        done(V.tensor_scalar(aux[:], M7[:], modA[:, 1:2], modA[:, 0:1], ALU.mult, ALU.add))
                    if h == 2 and p == 2:
                        settled().tensor_tensor(sqT[:], aux[:], aux[:], ALU.mult).then_inc(sq_rdy, 1)
                    if h == 3 and p == 0:
                        dve.wait_ge(ms_ps, b + 2)
                        V.tensor_scalar(nx[:, LN1], M7[:, 0:NT], 1.0 / P, RMS_EPS, ALU.mult,
                                        ALU.add).then_inc(ms_rdy, 1)
                    if h == 2 and p == 3:
                        V.tensor_single_scalar(upQ.bitcast(I32), aux[:].bitcast(I32), UPPER,
                                               ALU.bitwise_and).then_inc(hQ_up, 1)
                    if h == 8 and p == 0:
                        if live(b, h, 7):
                            dve.wait_ge(v_evac, HEADS * b + h + 8)
                        done(V.tensor_scalar(clamp[:], nx[:, LN1], NORM_MIN * NORM_MIN, None, ALU.mult))
                        V.tensor_copy(rV[:], ny[:, LN1]).then_inc(rV_rdy, 1)

                def behind(b, h, p):
                    if h == 2 and p == 0:
                        done(V.tensor_copy(modC[:], modT[:, :, bass.ds(b - 1, 1)].rearrange("p j b -> p (j b)")))
                    if h == 2 and p == 4:
                        dve.wait_ge(wo_ps, b)
                        settled().tensor_scalar(aT[:], ACC[:], modC[:, 2:3], None, ALU.mult).then_inc(aT_rdy, 1)
                    if h == 3:
                        if p == 0:
                            dve.wait_ge(at_ps, b)
                            dve.wait_ge(xr_ld, 16 * b)
                            V.tensor_tensor(x1[:].rearrange("p t d -> p (t d)"), ACC[:],
                                            x1[:].rearrange("p t d -> p (t d)"), ALU.add).then_inc(x1_sum, 1)
                            dve.wait_ge(x1_sum, b)
                            moments(x1, LN2)
                        places = ((), (0, 1), (2, 3), (), (4,), (5, 6, 7), (8, 9), ())
                        inverse_root(LN2, places[p])
                        if p == 7:
                            inverse_root(LN2, (10,))
                            settled()
                            for t in range(NT):
                                standardize(x1, LN2, t, x1_rdy)
                    if h == 5:
                        if p == 0:
                            dve.wait_ge(h2_rdy, b)
                            V.tensor_single_scalar(up2.bitcast(I32), h2T[:].bitcast(I32), UPPER,
                                                   ALU.bitwise_and).then_inc(h2_up, 1)
                        if p == 0 and first(b - 1):
                            dve.wait_ge(ld_eb, 16)
                        if p == 0:
                            dve.wait_ge(lg_ex, b)
                        for step in ((0,), (1,), (2,), (), (3, 4), (5,), (), (6,))[p]:
                            route(step)
                    if h == FFN0:
                        for step in ((), (7,), (8, 9), (), (10, 11), (12, 13), (), ())[p]:
                            route(step)
                    if h == FFN0 + 1 and p == 3:
                        dve.wait_ge(ct_ps, b)
                        V.tensor_copy(cT_sb[0:2 * E, :], C16[0:2 * E, 0:SEQ]).then_inc(cT_rdy, 1)

                def route(step):
                    tie, runs = eq[:, 0], (eq[:, 1], eq[:, 2])
                    now = slice(E, 2 * E)
                    v = scb[:].rearrange("p t (g c) -> p (t g) c", c=EG)
                    f = gs[:].rearrange("p t g -> p (t g)")
                    if step == 0:
                        done(settled().tensor_scalar(ex[:], ex[:], 1.0, None, ALU.add))
                    if step == 1:
                        done(settled().reciprocal(sco[:], ex[:]))
                        done(settled().tensor_tensor(scb[:], sco[:], eb_sb[:].unsqueeze(1).to_broadcast((P, NT, E)),
                                                     ALU.add))
                    if step == 2:
                        settled()
                        done(V.tensor_tensor(g1[:, :, 0:3], v[:, :, 0:3], v[:, :, 1:4], ALU.add))
                        done(V.tensor_tensor(g1[:, :, 3:5], v[:, :, 0:2], v[:, :, 2:4], ALU.add))
                        done(V.tensor_tensor(g1[:, :, 5], v[:, :, 0], v[:, :, 3], ALU.add))
                    if step == 3:
                        done(settled().tensor_reduce(f, g1[:], AX_X, ALU.max))
                        own = gs[:].unsqueeze(3).to_broadcast((P, NT, NG, NG))
                        other = gs[:].unsqueeze(2).to_broadcast((P, NT, NG, NG))
                        b4 = bt[:].rearrange("p (t g) a o -> p t g a o", g=NG)
                        settled()
                        done(V.tensor_tensor(b4[:, :, :, 0], other, own, ALU.is_gt))
                        done(V.tensor_tensor(b4[:, :, :, 1], other, own, ALU.is_equal))
                        done(settled().tensor_tensor(b4[:, :, :, 1], b4[:, :, :, 1],
                                                     lt[:].unsqueeze(1).to_broadcast((P, NT, NG, NG)), ALU.mult))
                    if step == 4:
                        done(settled().tensor_reduce(gm[:].rearrange("p t g -> p (t g)"),
                                                     bt[:].rearrange("p n a o -> p n (a o)"), AX_X, ALU.add))
                        done(settled().scalar_tensor_tensor(v, gm[:].rearrange("p t g -> p (t g)").unsqueeze(2)
                                                            .to_broadcast((P, NT * NG, EG)), float(TOPG), v,
                                                            ALU.is_lt, ALU.mult))
                    if step == 5:
                        settled(alone=True)
                        for t in range(NT):
                            done(V.max(top[:, t, :], scb[:, t, :]))
                        fourth = top[:, :, TOPK - 1:TOPK].to_broadcast((P, NT, E))
                        settled()
                        done(V.tensor_tensor(sel[:], scb[:], fourth, ALU.is_gt))
                        done(V.tensor_tensor(tie[:, :, now], scb[:], fourth, ALU.is_equal))
                    if step == 6:
                        settled()
                        done(V.tensor_reduce(need[:], sel[:], AX_X, ALU.add))
                        done(V.tensor_tensor(runs[0][:, :, now], tie[:, :, now], tie[:, :, E - 1:2 * E - 1], ALU.add))
                        done(settled().tensor_tensor(runs[1][:, :, now], runs[0][:, :, now],
                                                     runs[0][:, :, E - 2:2 * E - 2], ALU.add))
                    if step == 7:
                        done(settled().tensor_tensor(runs[0][:, :, now], runs[1][:, :, now],
                                                     runs[1][:, :, E - 4:2 * E - 4], ALU.add))
                    if step == 8:
                        done(settled().tensor_tensor(runs[1][:, :, now], runs[0][:, :, now],
                                                     runs[0][:, :, E - 8:2 * E - 8], ALU.add))
                        done(settled().tensor_tensor(runs[1][:, :, now], runs[1][:, :, now],
                                                     need[:].unsqueeze(2).to_broadcast((P, NT, E)), ALU.add))
                    if step == 9:
                        done(settled().scalar_tensor_tensor(cmb[:], runs[1][:, :, now], float(TOPK), tie[:, :, now],
                                                            ALU.is_le, ALU.mult))
                    if step == 10:
                        done(settled().tensor_tensor(sel[:], sel[:], cmb[:], ALU.add))
                        done(settled().tensor_tensor(cmb[:], sel[:], sco[:], ALU.mult))
                    if step == 11:
                        done(settled().tensor_reduce(need[:], cmb[:], AX_X, ALU.add))
                        done(settled().tensor_scalar(need[:], need[:], 1e-20, 1.0 / ROUTE_SCALE, ALU.add, ALU.mult))
                    if step == 12:
                        done(settled().reciprocal(need[:], need[:]))
                        done(settled().tensor_tensor(cmb[:], cmb[:], need[:].unsqueeze(2).to_broadcast((P, NT, E)),
                                                     ALU.mult))
                    if step == 13:
                        done(settled().tensor_copy(cs[:, :, 0, :], cmb[:]))
                        settled().tensor_tensor(cs[:, :, 1, :], cmb[:], cs[:, :, 0, :], ALU.subtract).then_inc(cs_rdy, 1)

                run(dve, slot, last_features, segment)


def kernel(**inputs):
    import numpy as _np
    import concourse.bacc as _bacc
    from concourse import mybir as _mybir
    from concourse.bass_utils import run_bass_kernel_spmd as _run

    a = {k.removeprefix("L0_"): _np.asarray(v) for k, v in inputs.items()}
    cat = _np.concatenate
    arrays = {
        "x": a["attn_tokens"],
        "wqkv": cat([a["attn_Wq"].reshape(P, 1, GROUPS, GW), a["attn_Wkv"].reshape(P, 2, GROUPS, GW)],
                    axis=1).transpose(0, 2, 1, 3).reshape(P, GROUPS, 3 * GW),
        "wo": a["attn_Wo"].reshape(PAIRS, P, P).transpose(1, 0, 2),
        "wg": cat([a["ffn_gate_w"].reshape(-1, P), a["ffn_sh_gate_w"]]).reshape(NJ, P, P).transpose(2, 0, 1),
        "wu": cat([a["ffn_up_w"].reshape(-1, P), a["ffn_sh_up_w"]]).reshape(NJ, P, P).transpose(2, 0, 1),
        "wd": cat([a["ffn_down_w"].transpose(0, 2, 1).reshape(-1, P), a["ffn_sh_down_w"].T])
        .reshape(NJ, P, P).transpose(1, 0, 2),
        "wr": a["ffn_router_weight"].T,
        "gq": a["attn_q_gamma"].reshape(1, HD),
        "gk": a["attn_k_gamma"].reshape(1, HD),
        "nw": a["attn_norm_w"].reshape(P, 1),
        "ebias": a["ffn_e_bias"].reshape(1, E),
        "cT": a["c"].T,
        "wmod": a["wmod"].reshape(P, 6, P),
    }
    nc = _bacc.Bacc("TRN2", target_bir_lowering=False, num_devices=1)
    given, args = {}, []
    for name, v in arrays.items():
        v = _np.ascontiguousarray(v)
        given[f"in_{name}"] = v
        args.append(nc.dram_tensor(f"in_{name}", v.shape, _mybir.dt.from_np(v.dtype), kind="ExternalInput").ap())
    args.append(nc.dram_tensor("out_0", (NB, SEQ, P), F32, kind="ExternalOutput").ap())
    block_kernel(nc, *args)
    r = _run(nc, [given], core_ids=[0])
    return r.results[0]["out_0"]
```
